# Optimizing a Trainium2 kernel written in Bass

```python
import numpy as np
import jax
import jax.numpy as jnp

def _softmax(x, axis=-1):
    return jax.nn.softmax(x, axis=axis)

def _gelu(x):
    return jax.nn.gelu(x, approximate=True)

def _silu(x):
    return jax.nn.silu(x)

def _sigmoid(x):
    return jax.nn.sigmoid(x)

def _layernorm(x, axis=-1, eps=1e-05):
    m = jnp.mean(x, axis=axis, keepdims=True)
    v = jnp.var(x, axis=axis, keepdims=True)
    return (x - m) / jnp.sqrt(v + eps)

def _scatter_add(tgt, idx, src, axis=0):
    return tgt.at[idx].add(src)

def _segment_sum(src, seg, n):
    return jax.ops.segment_sum(src, seg, n)
kernel_name = 'mk_vit_tower_d1_tok_img512_r4_93eed6'

def setup_inputs(seed: int=0):
    np.random.seed(seed)
    _w = jnp.asarray

    def _rec_inputs():
        import jax
        import jax.numpy as jnp
        _rk = jax.random.key(seed)
        x = -0.000356955 + 1 * jax.random.normal(jax.random.fold_in(_rk, 1), (16, 3, 96, 96), jnp.float32)
        return x
    x = _rec_inputs()

    def _L0_tok_setup():
        import jax, jax.numpy as jnp
        import numpy as np
        key = jax.random.key(seed)
        k1, k2, k3 = jax.random.split(key, 3)
        B, C, H, W = (128, 3, 224, 224)
        E, p = (128, 16)
        K = C * p * p
        img = jax.random.normal(k1, (B, C, H, W), dtype=jnp.float32)
        w = jax.random.normal(k2, (E, K), dtype=jnp.float32) * (1.0 / np.sqrt(K))
        b = jax.random.normal(k3, (E,), dtype=jnp.float32)
        return {'img': img, 'w': w, 'b': b, 'patch_size': p}
    _L0_tok_all = _L0_tok_setup()
    _L0_tok_in = {k: v for k, v in _L0_tok_all.items() if k in ('w', 'b')}
    del _L0_tok_all

    def _L0_attn_setup():
        import jax, jax.numpy as jnp
        import numpy as np
        B, N, DIM, HEADS, DH = (2, 512, 128, 8, 64)
        DIM_INNER = HEADS * DH
        SCALE = DH ** (-0.5)

        def _split_heads(t):
            b, n, _ = t.shape
            return t.reshape(b, n, HEADS, DH).transpose(0, 2, 1, 3)
        key = jax.random.key(seed)
        ks = jax.random.split(key, 8)
        w = lambda k: jax.random.normal(k, (DIM, DIM_INNER), dtype=jnp.float32) * 0.02
        return {'x': jax.random.normal(ks[0], (B, N, DIM), dtype=jnp.float32), 'w_q_u': w(ks[1]), 'w_k_u': w(ks[2]), 'w_v_u': w(ks[3]), 'w_q_c': w(ks[4]), 'w_k_c': w(ks[5]), 'w_v_c': w(ks[6]), 'w_out': jax.random.normal(ks[7], (DIM_INNER, DIM), dtype=jnp.float32) * 0.02}
    _L0_attn_all = _L0_attn_setup()
    _L0_attn_in = {k: v for k, v in _L0_attn_all.items() if k in ('w_q_u', 'w_k_u', 'w_v_u', 'w_q_c', 'w_k_c', 'w_v_c', 'w_out')}
    del _L0_attn_all

    def _L0_ffn_setup():
        import jax, jax.numpy as jnp
        import numpy as np
        K = 2
        key = jax.random.key(seed)
        ks = jax.random.split(key, 6)
        B, T, d, E, dff = (2, 512, 128, 8, 512)
        x = jax.random.normal(ks[0], (B, T, d), dtype=jnp.float32)
        Wg = jax.random.normal(ks[1], (d, E), dtype=jnp.float32) * 0.02
        W1 = jax.random.normal(ks[2], (E, d, dff), dtype=jnp.float32) * 0.02
        b1 = jnp.zeros((E, dff), dtype=jnp.float32)
        W2 = jax.random.normal(ks[3], (E, dff, d), dtype=jnp.float32) * 0.02
        b2 = jnp.zeros((E, d), dtype=jnp.float32)
        return {'x': x, 'Wg': Wg, 'W1': W1, 'b1': b1, 'W2': W2, 'b2': b2}
    _L0_ffn_all = _L0_ffn_setup()
    _L0_ffn_in = {k: v for k, v in _L0_ffn_all.items() if k in ('Wg', 'W1', 'b1', 'W2', 'b2')}
    del _L0_ffn_all
    return {'x': x, 'L0_tok_w': _L0_tok_in['w'], 'L0_tok_b': _L0_tok_in['b'], 'L0_attn_w_q_u': _L0_attn_in['w_q_u'], 'L0_attn_w_k_u': _L0_attn_in['w_k_u'], 'L0_attn_w_v_u': _L0_attn_in['w_v_u'], 'L0_attn_w_q_c': _L0_attn_in['w_q_c'], 'L0_attn_w_k_c': _L0_attn_in['w_k_c'], 'L0_attn_w_v_c': _L0_attn_in['w_v_c'], 'L0_attn_w_out': _L0_attn_in['w_out'], 'L0_ffn_Wg': _L0_ffn_in['Wg'], 'L0_ffn_W1': _L0_ffn_in['W1'], 'L0_ffn_b1': _L0_ffn_in['b1'], 'L0_ffn_W2': _L0_ffn_in['W2'], 'L0_ffn_b2': _L0_ffn_in['b2']}

def reference(x, L0_tok_w, L0_tok_b, L0_attn_w_q_u, L0_attn_w_k_u, L0_attn_w_v_u, L0_attn_w_q_c, L0_attn_w_k_c, L0_attn_w_v_c, L0_attn_w_out, L0_ffn_Wg, L0_ffn_W1, L0_ffn_b1, L0_ffn_W2, L0_ffn_b2):
    import jax
    import jax.numpy as jnp

    def _L0_tok_ref(img, w, b, patch_size):
        import jax, jax.numpy as jnp
        import numpy as np
        B, C, H, W = img.shape
        p = patch_size
        Hp, Wp = (H // p, W // p)
        S = Hp * Wp
        patches = img.reshape(B, C, Hp, p, Wp, p)
        patches = patches.transpose(0, 2, 4, 1, 3, 5).reshape(B, S, C * p * p)
        out = jnp.einsum('bsk,ek->bse', patches, w) + b
        return out

    def _L0_attn_ref(x, w_q_u, w_k_u, w_v_u, w_q_c, w_k_c, w_v_c, w_out):
        import jax, jax.numpy as jnp
        import numpy as np
        B, N, DIM, HEADS, DH = (2, 512, 128, 8, 64)
        DIM_INNER = HEADS * DH
        SCALE = DH ** (-0.5)

        def _split_heads(t):
            b, n, _ = t.shape
            return t.reshape(b, n, HEADS, DH).transpose(0, 2, 1, 3)
        b, n, _ = x.shape
        Qu, Ku, Vu = (_split_heads(x @ w) for w in (w_q_u, w_k_u, w_v_u))
        Qc, Kc, Vc = (_split_heads(x @ w) for w in (w_q_c, w_k_c, w_v_c))
        i = jnp.arange(n)[:, None]
        j = jnp.arange(n)[None, :]
        neg_inf = jnp.float32(-jnp.inf)
        causal_mask = jnp.where(j > i, neg_inf, 0.0)
        lookahead_mask = jnp.where(j <= i, neg_inf, 0.0)
        binary_causal = (j <= i).astype(x.dtype)
        term1 = jnp.einsum('bhid,bhjd->bhij', Qc, Vu) * SCALE * binary_causal
        sigmoid_term = jax.nn.sigmoid(jnp.einsum('bhid,bhjd->bhij', Qu, Ku) * SCALE + lookahead_mask)
        S_u = jnp.einsum('bhij,bhkj->bhik', term1, sigmoid_term)
        S_c = jnp.einsum('bhid,bhjd->bhij', Qc, Kc) * SCALE + causal_mask
        final_scores = S_c - jax.nn.silu(S_u)
        attn = jax.nn.softmax(final_scores, axis=-1)
        out = jnp.einsum('bhij,bhjd->bhid', attn, Vc)
        out = out.transpose(0, 2, 1, 3).reshape(b, n, DIM_INNER)
        return out @ w_out

    def _L0_ffn_ref(x, Wg, W1, b1, W2, b2):
        import jax, jax.numpy as jnp
        import numpy as np
        K = 2
        logits = jnp.einsum('btd,de->bte', x, Wg)
        probs = jax.nn.softmax(logits, axis=-1)
        top_p, _top_i = jax.lax.top_k(probs, K)
        top_p = top_p / jnp.sum(top_p, axis=-1, keepdims=True)
        b2_sum = jnp.sum(b2, axis=0)
        out = jnp.zeros_like(x)
        for i in range(K):
            w_in = x * top_p[..., i:i + 1]
            h = jax.nn.gelu(jnp.einsum('btd,edf->ebtf', w_in, W1) + b1[:, None, None, :], approximate=False)
            out = out + jnp.einsum('ebtf,efd->btd', h, W2) + b2_sum
        return out
    h = _L0_tok_ref(x, L0_tok_w, L0_tok_b, 16)
    h = h + _L0_attn_ref(_layernorm(h, axis=-1), L0_attn_w_q_u, L0_attn_w_k_u, L0_attn_w_v_u, L0_attn_w_q_c, L0_attn_w_k_c, L0_attn_w_v_c, L0_attn_w_out)
    h = h + _L0_ffn_ref(_layernorm(h, axis=-1), L0_ffn_Wg, L0_ffn_W1, L0_ffn_b1, L0_ffn_W2, L0_ffn_b2)
    return h

_drawn_inputs = setup_inputs


def setup_inputs(seed=0):
    import zlib

    import numpy as np

    out = dict(_drawn_inputs(seed))
    spreads = {'L0_ffn_b1': (0.0, 0.1), 'L0_ffn_b2': (0.0, 0.1)}
    factors = {'L0_attn_w_q_u': 133.988,
     'L0_attn_w_k_u': 124.125,
     'L0_attn_w_v_u': 73.304,
     'L0_attn_w_q_c': 8.0,
     'L0_attn_w_k_c': 8.0,
     'L0_ffn_Wg': 200.0}
    for name, (base, spread) in spreads.items():
        noise = np.random.default_rng([zlib.crc32(name.encode()), seed]).standard_normal(out[name].shape)
        drawn = base * np.exp(spread * noise) if base else spread * noise
        out[name] = jnp.asarray(drawn.astype(out[name].dtype))
    for name, factor in factors.items():
        out[name] = (out[name] * factor).astype(out[name].dtype)
    return out
```

```python
from contextlib import ExitStack

import concourse.bass as bass
from concourse import mybir

P = 128
F32 = mybir.dt.float32
F32R = mybir.dt.float32r
ALU = mybir.AluOpType
ACT = mybir.ActivationFunctionType
AX_X = mybir.AxisListType.X
EPS = 1e-5
NEG = -1e30

QU, KU, VU, QC, KC, VC = range(6)


def vit_layer(nc, patches, tok_w, consts, small, w_qkv, w_out, w1, w2, out, dims):
    B, S, D, HEADS, DH, E, DFF, KP = (dims[k] for k in ("B", "S", "D", "HEADS", "DH", "E", "DFF", "KP"))
    T = B * S
    HT = T // 2
    CH = HEADS * DH // P
    CF = DFF // P
    NB = 4
    NG = B // NB
    GT = NB * S
    ROWS = 64 + S
    BLK = CH * (NB // 2)
    WIDE = BLK * S
    TT = 96
    NT = T // TT
    NCH = E * CF
    SCALE = float(DH) ** -0.5
    assert D == P and DH == 64 and S <= 64 and WIDE <= 512 and HT <= 512 and NT * TT == T and CF == 4

    with ExitStack() as ctx:
        def sb(name, shape, dt=F32):
            return ctx.enter_context(nc.sbuf_tensor(name, shape, dt))

        def sem(name):
            return ctx.enter_context(nc.semaphore(name))

        ps = ctx.enter_context(nc.psum_tensor("ps", [P, 8, 512], F32))

        patch_sb = sb("patch_sb", [P, KP, T])
        tok_w_sb = sb("tok_w_sb", [P, KP, D])
        const_sb = sb("const_sb", [P, 2 * P + 3 * S])
        small_sb = sb("small_sb", [P, 1 + 2 * E + E * CF])
        center = const_sb[:, 0:P]
        ident = const_sb[:, P:2 * P]
        tok_b = small_sb[:, 0:1]
        b2_sb = small_sb[:, 1:1 + E]
        w_gate = small_sb[:, 1 + E:1 + 2 * E]
        b1_sb = small_sb[:, 1 + 2 * E:1 + 2 * E + E * CF]
        w_qkv_sb = sb("w_qkv_sb", [P, 6, CH * P])
        w_qkv_hi = sb("w_qkv_hi", [P, 6, CH * P], F32R)
        w_qkv_lo = sb("w_qkv_lo", [P, 6, CH * P], F32R)
        w_out_sb = sb("w_out_sb", [P, CH, D])
        w1_sb = sb("w1_sb", [P, E * DFF])
        w2_sb = sb("w2_sb", [P, E * DFF])
        mean_w = sb("mean_w", [P, P])
        ones = sb("ones", [P, P])
        eps = sb("eps", [P, 1])
        masks = sb("masks", [P, 3, BLK, S])
        gate_mask, look_mask, causal_mask = (masks[0:ROWS, k].rearrange("p n s -> p (n s)") for k in range(3))

        h0 = sb("h0", [P, 2, HT])
        h1 = sb("h1", [P, 2, HT])
        sq = sb("sq", [P, 2, HT])
        xc = sb("xc", [P, 2, HT])
        sd = sb("sd", [P, NT])
        rstd = sb("rstd", [P, NT])
        xn = sb("xn", [P, T])
        xn2 = sb("xn2", [P, T])

        x_hi = sb("x_hi", [P, NB, 64], F32R)
        x_lo = sb("x_lo", [P, NB, 64], F32R)
        qk = sb("qk", [P, 5, CH, GT])
        v_sb = sb("v_sb", [P, NB // 2, CH * P])
        gate = sb("gate", [P, 2, WIDE])
        look_t = sb("look_t", [P, 2, WIDE])
        look = sb("look", [P, 2, WIDE])
        sc_m = sb("sc_m", [P, 2, WIDE])
        su_t = sb("su_t", [P, 2, WIDE])
        su = sb("su", [P, 2, WIDE])
        logit = sb("logit", [P, 2, WIDE])
        shifted = sb("shifted", [P, 2, WIDE])
        expd = sb("expd", [P, 2, WIDE])
        prob = sb("prob", [P, 2, WIDE])
        prob_t = sb("prob_t", [P, 2, WIDE])
        row_max = sb("row_max", [P, 2 * BLK])
        row_sum = sb("row_sum", [P, 2 * BLK])
        row_inv = sb("row_inv", [P, 2 * BLK])
        o_t = sb("o_t", [P, CH, T])

        g_max = sb("g_max", [P, NT])
        g_shift = sb("g_shift", [P, NT, E])
        g_exp = sb("g_exp", [P, NT, E])
        g_sum = sb("g_sum", [P, NT])
        g_inv = sb("g_inv", [P, NT])
        g_prob = sb("g_prob", [P, NT, E])
        g_top = sb("g_top", [P, NT, 8])
        g_two = sb("g_two", [P, NT])
        g_twoi = sb("g_twoi", [P, NT])
        g_pn = sb("g_pn", [P, 2, NT])
        g_p0i = sb("g_p0i", [P, NT])
        g_ratio = sb("g_ratio", [P, NT])
        diag = sb("diag", [P, 2, NT, TT])
        xs = sb("xs", [P, 2, HT])
        xs_hi = sb("xs_hi", [P, 2, HT], F32R)
        xs_lo = sb("xs_lo", [P, 2, HT], F32R)
        ratio = sb("ratio", [P, 2, HT])

        w1_hi = sb("w1_hi", [P, 2, 2 * P], F32R)
        w1_lo = sb("w1_lo", [P, 2, 2 * P], F32R)
        w2_hi = sb("w2_hi", [P, 2, 2 * P], F32R)
        w2_lo = sb("w2_lo", [P, 2, 2 * P], F32R)
        zb = sb("zb", [P, 2, 2, HT])
        ga = sb("ga", [P, 2, 2, HT])
        gb = sb("gb", [P, 2, 2, HT])
        hid = sb("hid", [P, 2, 2, HT])
        hid_hi = sb("hid_hi", [P, 2, 2, HT], F32R)
        hid_lo = sb("hid_lo", [P, 2, 2, HT], F32R)
        b2_sum = sb("b2_sum", [P, 1])
        b2_twice = sb("b2_twice", [P, 1])
        y = xs

        tokw_in, const_in, small_in = sem("tokw_in"), sem("const_in"), sem("small_in")
        patch_in = [sem(f"patch_in{k}") for k in range(KP)]
        qkv_in = [sem(f"qkv_in{k}") for k in range(6)]
        wout_in, w1_in, w2_in = sem("wout_in"), sem("w1_in"), sem("w2_in")
        stored = sem("stored")
        fills, masks_ready, xpads_ready = sem("fills"), sem("masks_ready"), sem("xpads_ready")
        qkv_hi_ready, qkv_split = sem("qkv_hi_ready"), sem("qkv_split")
        emb_done, res_ready = sem("emb_done"), sem("res_ready")
        cen_done, xc_ready, sq_ready, var_done, sd_ready, rstd_ready, ndiag_ready, norm_mm, xn_ready = (
            sem("cen_done"), sem("xc_ready"), sem("sq_ready"), sem("var_done"), sem("sd_ready"), sem("rstd_ready"),
            sem("ndiag_ready"), sem("norm_mm"), sem("xn_ready"))
        xhi_ready, x_split = sem("xhi_ready"), sem("x_split")
        qk_done, qk_by_act, qk_by_dve, vp_done, v_ready = (
            sem("qk_done"), sem("qk_by_act"), sem("qk_by_dve"), sem("vp_done"), sem("v_ready"))
        gate_done, look_done, sc_done, su_done = sem("gate_done"), sem("look_done"), sem("sc_done"), sem("su_done")
        gate_ready, lookt_ready, look_ready, scm_ready = (
            sem("gate_ready"), sem("lookt_ready"), sem("look_ready"), sem("scm_ready"))
        sut_ready, logit_ready, max_ready, shift_ready, exp_ready, sum_ready, inv_ready, prob_ready = (
            sem("sut_ready"), sem("logit_ready"), sem("max_ready"), sem("shift_ready"),
            sem("exp_ready"), sem("sum_ready"), sem("inv_ready"), sem("prob_ready"))
        pt_done, pv_done = sem("pt_done"), sem("pv_done")
        gate_free, look_free, score_free = sem("gate_free"), sem("look_free"), sem("score_free")
        proj_done = sem("proj_done")
        route_mm, route_step, route_exp, diag_ready, share_mm = (
            sem("route_mm"), sem("route_step"), sem("route_exp"), sem("diag_ready"), sem("share_mm"))
        xs_ready, xshi_ready, xs_split, ratio_ready = sem("xs_ready"), sem("xshi_ready"), sem("xs_split"), sem("ratio_ready")
        w1hi_ready, w1_split, w2hi_ready, w2_split = sem("w1hi_ready"), sem("w1_split"), sem("w2hi_ready"), sem("w2_split")
        up_done, down_done, zb_ready, ga_ready, gb_ready, hid_ready, hhi_ready, hid_split = (
            sem("up_done"), sem("down_done"), sem("zb_ready"), sem("ga_ready"), sem("gb_ready"),
            sem("hid_ready"), sem("hhi_ready"), sem("hid_split"))
        b2s_ready, b2_ready, y_ready = sem("b2s_ready"), sem("b2_ready"), sem("y_ready")

        def pair(b, n):
            return ps[:, b:b + 2, 0:n]

        emb_ps, cen_ps, norm_ps = pair(0, HT), pair(2, HT), pair(6, HT)
        var_ps = ps[0:TT, 4:6, 0:NT // 2]
        gate_ps, look_ps, sc_ps = pair(2, WIDE), pair(4, WIDE), pair(6, WIDE)
        su_ps, pt_ps, o_ps = gate_ps, look_ps, sc_ps
        attn_ps = pair(0, HT)
        route_ps = ps[0:TT, 4, 0:NT * E].rearrange("p (n e) -> p n e", n=NT)
        share_ps, ratio_ps = pair(6, HT), pair(0, HT)
        down_ps, up_ps = pair(0, HT), (pair(2, HT), pair(4, HT))

        def split_mm(pe, dst, w, w_lo, x, x_lo, first=True, last=True):
            pe.matmul(dst, w, x, start=first, stop=False)
            pe.matmul(dst, w_lo, x, start=False, stop=False)
            return pe.matmul(dst, w, x_lo, start=False, stop=last)

        block = ctx.enter_context(nc.Block())

        @block.tensor
        def _(pe):
            def layer_norm(k):
                res = h0 if k == 0 else h1
                if k == 0:
                    pe.wait_ge(const_in, 16)
                    pe.wait_ge(fills, 2)
                for half in range(2):
                    pe.wait_ge(res_ready, 2 * k + half + 1)
                    pe.matmul(cen_ps[:, half], center, res[:, half], start=True, stop=True).then_inc(cen_done, 1)
                for half in range(2):
                    pe.wait_ge(sq_ready, 2 * k + half + 1)
                    for n in range(NT // 2):
                        mm = pe.matmul(var_ps[:, half, n:n + 1], sq[:, half, n * TT:(n + 1) * TT], mean_w[:, 0:1],
                                       start=True, stop=True)
                    mm.then_inc(var_done, 1)
                for half in range(2):
                    pe.wait_ge(ndiag_ready, 2 * k + half + 1)
                    spread(norm_ps, 0, half).then_inc(norm_mm, 1)

            def spread(dst, k, half):
                tiles = slice(half * NT // 2, (half + 1) * NT // 2)
                return pe.matmul(dst[:, half], ones[0:TT, :], diag[0:TT, k, tiles].rearrange("p n t -> p (n t)"),
                                 start=True, stop=True)

            pe.wait_ge(tokw_in, 16)
            for k in range(KP):
                pe.wait_ge(patch_in[k], 16)
                for half in range(2):
                    mm = pe.matmul(emb_ps[:, half], tok_w_sb[:, k], patch_sb[:, k, half * HT:(half + 1) * HT],
                                   start=(k == 0), stop=(k == KP - 1))
                    if k == KP - 1:
                        mm.then_inc(emb_done, 1)
            for free in (gate_free, look_free, score_free):
                pe.wait_ge(free, 1)
            layer_norm(0)

            def project_qk(g):
                pe.wait_ge(x_split, g + 1)
                for m in range(5):
                    if isinstance(g, int) and g == 0:
                        pe.wait_ge(qkv_split, m + 1)
                    for n in range(2):
                        part = 2 * m + n
                        if part >= 2:
                            pe.wait_ge(qk_by_act if n == 0 else qk_by_dve, 5 * g + m)
                        elif not (isinstance(g, int) and g == 0):
                            pe.wait_ge(v_ready, 2 * g)
                        for c in range(2):
                            ch = slice((2 * n + c) * P, (2 * n + c + 1) * P)
                            mm = split_mm(pe, ps[:, n, c * GT:(c + 1) * GT], w_qkv_hi[:, m, ch], w_qkv_lo[:, m, ch],
                                          x_hi[:, :, 0:S], x_lo[:, :, 0:S])
                        mm.then_inc(qk_done, 1)

            def project_v(g):
                if isinstance(g, int) and g == 0:
                    pe.wait_ge(qkv_split, 6)
                for q in range(2):
                    pe.wait_ge(qk_by_act if q == 0 else qk_by_dve, 5 * g + 5)
                    two = slice(2 * q, 2 * q + 2)
                    split_mm(pe, ps[:, q, :], x_hi[:, two].rearrange("p b s -> p (b s)"),
                             x_lo[:, two].rearrange("p b s -> p (b s)"),
                             w_qkv_hi[:, VC], w_qkv_lo[:, VC]).then_inc(vp_done, 1)

            def by_head(dst, a, b):
                for blk in range(BLK):
                    c, q = divmod(blk, NB // 2)
                    for hp in range(2):
                        for bp in range(2):
                            cols = slice((2 * q + bp) * S, (2 * q + bp + 1) * S)
                            rows = slice(64 * hp, 64 * hp + 64)
                            mm = pe.matmul(dst[64 * bp:64 * bp + S, hp, blk * S:(blk + 1) * S],
                                           qk[rows, a, c, cols], qk[rows, b, c, cols], start=True, stop=True)
                return mm

            def scores(g):
                pe.wait_ge(qk_by_act, 5 * g + 5)
                pe.wait_ge(qk_by_dve, 5 * g + 5)
                pe.wait_ge(gate_free, g + 1)
                pe.nop(nofuse=True)
                by_head(gate_ps, VU, QC).then_inc(gate_done, 1)
                pe.wait_ge(look_free, 2 * g + 1)
                pe.nop(nofuse=True)
                by_head(look_ps, KU, QU).then_inc(look_done, 1)
                pe.wait_ge(score_free, 2 * g + 1)
                pe.nop(nofuse=True)
                by_head(sc_ps, QC, KC).then_inc(sc_done, 1)
                pe.wait_ge(gate_ready, g + 1)
                pe.wait_ge(look_ready, g + 1)
                pe.nop(nofuse=True)
                for hp in range(2):
                    for blk in range(BLK):
                        for bp in range(2):
                            rows, cols = slice(64 * bp, 64 * bp + S), slice(blk * S, (blk + 1) * S)
                            mm = pe.matmul(su_ps[rows, hp, cols], gate[rows, hp, cols], look[rows, hp, cols],
                                           start=True, stop=True)
                mm.then_inc(su_done, 1)

            def transpose_probs(g):
                pe.wait_ge(prob_ready, g + 1)
                pe.nop(nofuse=True)
                for hp in range(2):
                    for blk in range(BLK):
                        for bp in range(2):
                            rows, cols = slice(64 * bp, 64 * bp + S), slice(blk * S, (blk + 1) * S)
                            mm = pe.matmul(pt_ps[rows, hp, cols], prob[rows, hp, cols], ident[rows, rows],
                                           start=True, stop=True)
                    mm.then_inc(pt_done, 1)

            def weighted_values(g):
                pe.wait_ge(v_ready, 2 * g + 2)
                pe.wait_ge(scm_ready, g + 1)
                for hp in range(2):
                    pe.wait_ge(look_free, 2 * g + hp + 2)
                    pe.nop(nofuse=True)
                    for blk in range(BLK):
                        c, q = divmod(blk, NB // 2)
                        head = slice((2 * c + hp) * 64, (2 * c + hp + 1) * 64)
                        for bp in range(2):
                            rows, cols = slice(64 * bp, 64 * bp + S), slice(blk * S, (blk + 1) * S)
                            mm = pe.matmul(o_ps[64 * hp:64 * hp + 64, bp, cols], v_sb[rows, q, head],
                                           prob_t[rows, hp, cols], start=True, stop=True)
                mm.then_inc(pv_done, 1)

            project_qk(0)
            project_v(0)
            with pe.Fori(0, NG - 1) as g:
                scores(g)
                project_qk(g + 1)
                project_v(g + 1)
                transpose_probs(g)
                weighted_values(g)
            scores(NG - 1)
            transpose_probs(NG - 1)
            weighted_values(NG - 1)

            pe.wait_ge(score_free, 2 * NG + 1)
            pe.wait_ge(wout_in, 16)
            for half in range(2):
                for c in range(CH):
                    mm = pe.matmul(attn_ps[:, half], w_out_sb[:, c], o_t[:, c, half * HT:(half + 1) * HT],
                                   start=(c == 0), stop=(c == CH - 1))
                mm.then_inc(proj_done, 1)
            layer_norm(1)

            pe.wait_ge(xn_ready, 4)
            for n in range(NT):
                mm = pe.matmul(route_ps[:, n], xn2[:, n * TT:(n + 1) * TT], w_gate, start=True, stop=True)
            mm.then_inc(route_mm, 1)
            for k, dst in enumerate((share_ps, ratio_ps)):
                pe.wait_ge(diag_ready, k + 1)
                for half in range(2):
                    mm = spread(dst, k, half)
                mm.then_inc(share_mm, 1)

            def up(e, c):
                n = e * CF + c
                slot, at = c // 2, slice((c % 2) * P, (c % 2 + 1) * P)
                pe.wait_ge(w1_split, 2 * e + slot + 1)
                if not (isinstance(n, int) and n < 2):
                    pe.wait_ge(zb_ready, n - 1)
                for half in range(2):
                    mm = split_mm(pe, up_ps[c % 2][:, half], w1_hi[:, slot, at], w1_lo[:, slot, at],
                                  xs_hi[:, half], xs_lo[:, half])
                mm.then_inc(up_done, 1)

            def down(e, c):
                n = e * CF + c
                slot, at = c // 2, slice((c % 2) * P, (c % 2 + 1) * P)
                first, last = isinstance(n, int) and n == 0, isinstance(n, int) and n == NCH - 1
                pe.wait_ge(w2_split, 2 * e + slot + 1)
                pe.wait_ge(hid_split, n + 1)
                for half in range(2):
                    mm = split_mm(pe, down_ps[:, half], w2_hi[:, slot, at], w2_lo[:, slot, at],
                                  hid_hi[:, c % 2, half], hid_lo[:, c % 2, half], first=first, last=last)
                mm.then_inc(down_done, 1)

            pe.wait_ge(xs_split, 1)
            for c in range(CF):
                up(0, c)
            pe.wait_ge(ratio_ready, 1)
            for c in range(CF):
                up(1, c)
                down(0, c)
            with pe.Fori(1, E - 1) as e:
                for c in range(CF):
                    up(e + 1, c)
                    down(e, c)
            for c in range(CF):
                down(E - 1, c)

        @block.scalar
        def _(act):
            act.wait_ge(small_in, 16)
            for half in range(2):
                act.wait_ge(emb_done, half + 1)
                nc.scalar.activation(h0[:, half], emb_ps[:, half], ACT.Identity, bias=tok_b).then_inc(res_ready, 1)

            def layer_norm(k):
                for half in range(2):
                    act.wait_ge(cen_done, 2 * k + half + 1)
                    nc.scalar.copy(xc[:, half], cen_ps[:, half]).then_inc(xc_ready, 1)
                act.wait_ge(var_done, 2 * k + 2)
                nc.scalar.activation(sd[0:TT, :].rearrange("p (h n) -> p h n", h=2), var_ps, ACT.Sqrt,
                                     bias=eps[0:TT]).then_inc(sd_ready, 1)

            act.wait_ge(fills, 3)
            layer_norm(0)
            nc.scalar.preload_act_table(ACT.Tanh)

            def take_qk(g):
                for m in range(5):
                    act.wait_ge(qk_done, 10 * g + 2 * m + 1)
                    nc.scalar.copy(qk[:, m, 0:2], ps[:, 0, 0:2 * GT].rearrange("p (c t) -> p c t", c=2))\
                        .then_inc(qk_by_act, 1)

            def take_v(g):
                for q in range(2):
                    act.wait_ge(vp_done, 2 * g + q + 1)
                    nc.scalar.copy(v_sb[:, q], ps[:, q, :]).then_inc(v_ready, 1)

            def tanhs(g):
                act.wait_ge(look_done, g + 1)
                nc.scalar.activation(look_t[0:ROWS], look_ps[0:ROWS], ACT.Tanh, scale=SCALE / 2)\
                    .then_inc(lookt_ready, 1)
                act.wait_ge(su_done, g + 1)
                nc.scalar.activation(su_t[0:ROWS], su_ps[0:ROWS], ACT.Tanh, scale=0.5).then_inc(sut_ready, 1)

            def softmax(g):
                act.wait_ge(shift_ready, g + 1)
                nc.scalar.activation(expd[0:ROWS], shifted[0:ROWS], ACT.Exp, scale=SCALE).then_inc(exp_ready, 1)
                for hp in range(2):
                    act.wait_ge(pt_done, 2 * g + hp + 1)
                    nc.scalar.copy(prob_t[0:ROWS, hp], pt_ps[0:ROWS, hp]).then_inc(look_free, 1)

            def take_o(g):
                act.wait_ge(pv_done, g + 1)
                act.nop(nofuse=True)
                for bp in range(2):
                    at = o_t[:].rearrange("p c (g q b s) -> p c g q b s", g=NG, b=2, s=S)
                    dst = at[:, :, bass.ds(g, 1) if not isinstance(g, int) else slice(g, g + 1), :, bp]
                    nc.scalar.copy(dst.rearrange("p c g q s -> p c (g q) s"),
                                   o_ps[:, bp].rearrange("p (c q s) -> p c q s", c=CH, s=S)).then_inc(score_free, 1)

            take_qk(0)
            take_v(0)
            with act.Fori(0, NG - 1) as g:
                tanhs(g)
                take_qk(g + 1)
                softmax(g)
                take_o(g)
                take_v(g + 1)
            tanhs(NG - 1)
            softmax(NG - 1)
            take_o(NG - 1)

            layer_norm(1)
            act.wait_ge(route_step, 2)
            nc.scalar.activation(g_exp[0:TT], g_shift[0:TT], ACT.Exp).then_inc(route_exp, 1)
            nc.scalar.preload_act_table(ACT.Gelu)

            def gelu_first(n, s):
                act.wait_ge(up_done, n + 1)
                if not (isinstance(n, int) and n < 2):
                    act.wait_ge(hid_ready, n - 1)
                act.nop(nofuse=True)
                nc.scalar.activation(ga[:, s], up_ps[s], ACT.Gelu, bias=b1_sb[:, bass.ds(n, 1)]).then_inc(ga_ready, 1)

            def gelu_second(n, s):
                act.wait_ge(zb_ready, n + 1)
                if not (isinstance(n, int) and n < 2):
                    act.wait_ge(hid_ready, n - 1)
                act.nop(nofuse=True)
                nc.scalar.activation(gb[:, s], zb[:, s], ACT.Gelu, bias=b1_sb[:, bass.ds(n, 1)]).then_inc(gb_ready, 1)

            def high_part(n, s):
                act.wait_ge(hid_ready, n + 1)
                if not (isinstance(n, int) and n < 2):
                    act.wait_ge(down_done, n - 1)
                nc.scalar.copy(hid_hi[:, s], hid[:, s]).then_inc(hhi_ready, 1)

            def step(n, s):
                gelu_first(n, s)
                if not (isinstance(n, int) and n < 1):
                    gelu_second(n - 1, 1 - s)
                if not (isinstance(n, int) and n < 2):
                    high_part(n - 2, s)

            for c in range(CF):
                step(c, c % 2)
            with act.Fori(1, E) as e:
                for c in range(CF):
                    step(e * CF + c, c % 2)
            gelu_second(NCH - 1, 1)
            high_part(NCH - 2, 0)
            high_part(NCH - 1, 1)

        @block.vector
        def _(dve):
            def both(ap):
                return ap[0:ROWS]

            def blocks(ap):
                return ap[0:ROWS].rearrange("p h (n s) -> p (h n) s", s=S)

            nc.vector.memset(mean_w[:], 1.0 / D).then_inc(fills, 1)
            nc.vector.memset(ones[:], 1.0).then_inc(fills, 1)
            nc.vector.memset(eps[:], EPS).then_inc(fills, 1)
            nc.vector.memset(x_hi[:].bitcast(F32), 0.0)
            nc.vector.memset(x_lo[:].bitcast(F32), 0.0).then_inc(xpads_ready, 1)
            for b, free in ((2, gate_free), (4, look_free), (6, score_free)):
                nc.vector.memset(ps[32:64, b:b + 2, 0:WIDE], 0.0).then_inc(free, 1)
            dve.wait_ge(const_in, 16)
            nc.vector.tensor_copy(
                masks[:], const_sb[:, 2 * P:].rearrange("p (k o s) -> p k o s", k=3, o=1).broadcast_to([P, 3, BLK, S]))\
                .then_inc(masks_ready, 1)
            dve.wait_ge(small_in, 16)
            nc.vector.reduce_sum(b2_sum[:], b2_sb, AX_X).then_inc(b2s_ready, 1)
            dve.wait_ge(b2s_ready, 1)
            nc.vector.tensor_scalar(b2_twice[:], b2_sum[:], 2.0, None, ALU.mult).then_inc(b2_ready, 1)

            def layer_norm(k, dst):
                for half in range(2):
                    dve.wait_ge(xc_ready, 2 * k + half + 1)
                    nc.vector.tensor_tensor(sq[:, half], xc[:, half], xc[:, half], ALU.mult).then_inc(sq_ready, 1)
                dve.wait_ge(sd_ready, k + 1)
                nc.vector.reciprocal(rstd[0:TT, :], sd[0:TT, :]).then_inc(rstd_ready, 1)
                dve.wait_ge(rstd_ready, k + 1)
                for half in range(2):
                    spread_out(0, rstd, half).then_inc(ndiag_ready, 1)
                for half in range(2):
                    dve.wait_ge(norm_mm, 2 * k + half + 1)
                    nc.vector.tensor_tensor(dst[:, half * HT:(half + 1) * HT], xc[:, half], norm_ps[:, half],
                                            ALU.mult).then_inc(xn_ready, 1)

            def spread_out(k, by_token, half):
                tiles = slice(half * NT // 2, (half + 1) * NT // 2)
                n = NT // 2
                return nc.vector.tensor_tensor(
                    diag[0:TT, k, tiles],
                    ident[0:TT, 0:TT].rearrange("p (o t) -> p o t", o=1).broadcast_to([TT, n, TT]),
                    by_token[0:TT, tiles].rearrange("p (n o) -> p n o", o=1).broadcast_to([TT, n, TT]), ALU.mult)

            layer_norm(0, xn)

            def split_x(g):
                dve.wait_ge(xpads_ready, 1)
                dve.wait_ge(xn_ready, 2)
                if not (isinstance(g, int) and g == 0):
                    dve.wait_ge(vp_done, 2 * g)
                x = xn[:, bass.ds(g * GT, GT)].rearrange("p (b s) -> p b s", b=NB)
                nc.vector.tensor_copy(x_hi[:, :, 0:S], x).then_inc(xhi_ready, 1)
                dve.wait_ge(xhi_ready, g + 1)
                nc.vector.tensor_tensor(x_lo[:, :, 0:S], x, x_hi[:, :, 0:S].bitcast(F32), ALU.subtract)\
                    .then_inc(x_split, 1)

            def take_qk(g, m):
                dve.wait_ge(qk_done, 10 * g + 2 * m + 2)
                nc.vector.tensor_copy(qk[:, m, 2:4], ps[:, 1, 0:2 * GT].rearrange("p (c t) -> p c t", c=2))\
                    .then_inc(qk_by_dve, 1)

            def over(mask):
                return mask.rearrange("p (o w) -> p o w", o=1).broadcast_to([ROWS, 2, WIDE])

            def attention(g, more):
                dve.wait_ge(gate_done, g + 1)
                nc.vector.tensor_tensor(both(gate), both(gate_ps), over(gate_mask), ALU.mult).then_inc(gate_ready, 1)
                dve.wait_ge(lookt_ready, g + 1)
                nc.vector.scalar_tensor_tensor(both(look), both(look_t), 1.0, over(look_mask), ALU.add, ALU.mult)\
                    .then_inc(look_ready, 1)
                dve.wait_ge(sc_done, g + 1)
                nc.vector.tensor_tensor(both(sc_m), both(sc_ps), over(causal_mask), ALU.add).then_inc(scm_ready, 1)
                if more:
                    split_x(g + 1)
                dve.wait_ge(sut_ready, g + 1)
                nc.vector.scalar_tensor_tensor(both(su), both(su_t), 1.0, both(su_ps), ALU.add, ALU.mult)\
                    .then_inc(gate_free, 1)
                dve.wait_ge(gate_free, g + 2)
                nc.vector.scalar_tensor_tensor(both(logit), both(su), -0.5 / SCALE, both(sc_m), ALU.mult, ALU.add)\
                    .then_inc(logit_ready, 1)
                if more:
                    take_qk(g + 1, 0)
                dve.wait_ge(logit_ready, g + 1)
                nc.vector.tensor_reduce(row_max[0:ROWS], blocks(logit), AX_X, ALU.max).then_inc(max_ready, 1)
                if more:
                    take_qk(g + 1, 1)
                dve.wait_ge(max_ready, g + 1)
                nc.vector.tensor_tensor(blocks(shifted), blocks(logit), wide(row_max), ALU.subtract)\
                    .then_inc(shift_ready, 1)
                if more:
                    take_qk(g + 1, 2)
                    take_qk(g + 1, 3)
                dve.wait_ge(exp_ready, g + 1)
                nc.vector.tensor_reduce(row_sum[0:ROWS], blocks(expd), AX_X, ALU.add).then_inc(sum_ready, 1)
                dve.wait_ge(sum_ready, g + 1)
                nc.vector.reciprocal(row_inv[0:ROWS], row_sum[0:ROWS]).then_inc(inv_ready, 1)
                dve.wait_ge(inv_ready, g + 1)
                nc.vector.tensor_tensor(blocks(prob), blocks(expd), wide(row_inv), ALU.mult).then_inc(prob_ready, 1)
                if more:
                    take_qk(g + 1, 4)

            def wide(rows):
                return rows[0:ROWS].rearrange("p (n o) -> p n o", o=1).broadcast_to([ROWS, 2 * BLK, S])

            split_x(0)
            for m in range(5):
                take_qk(0, m)
            dve.wait_ge(masks_ready, 1)
            with dve.Fori(0, NG - 1) as g:
                attention(g, True)
            attention(NG - 1, False)

            for half in range(2):
                dve.wait_ge(proj_done, half + 1)
                nc.vector.tensor_tensor(h1[:, half], attn_ps[:, half], h0[:, half], ALU.add).then_inc(res_ready, 1)
            layer_norm(1, xn2)

            steps = 0

            def done(ins):
                nonlocal steps
                steps += 1
                ins.then_inc(route_step, 1)
                dve.wait_ge(route_step, steps)

            def over_experts(v):
                return v[0:TT].rearrange("p (n o) -> p n o", o=1).broadcast_to([TT, NT, E])

            dve.wait_ge(route_mm, 1)
            done(nc.vector.tensor_reduce(g_max[0:TT], route_ps, AX_X, ALU.max))
            done(nc.vector.tensor_tensor(g_shift[0:TT], route_ps, over_experts(g_max), ALU.subtract))
            dve.wait_ge(route_exp, 1)
            done(nc.vector.tensor_reduce(g_sum[0:TT], g_exp[0:TT], AX_X, ALU.add))
            done(nc.vector.reciprocal(g_inv[0:TT], g_sum[0:TT]))
            done(nc.vector.tensor_tensor(g_prob[0:TT], g_exp[0:TT], over_experts(g_inv), ALU.mult))
            for n in range(NT - 1):
                nc.vector.max(g_top[0:TT, n], g_prob[0:TT, n])
            done(nc.vector.max(g_top[0:TT, NT - 1], g_prob[0:TT, NT - 1]))
            done(nc.vector.tensor_tensor(g_two[0:TT], g_top[0:TT, :, 0], g_top[0:TT, :, 1], ALU.add))
            done(nc.vector.reciprocal(g_twoi[0:TT], g_two[0:TT]))
            for k in range(2):
                done(nc.vector.tensor_tensor(g_pn[0:TT, k], g_top[0:TT, :, k], g_twoi[0:TT], ALU.mult))
            for half in range(2):
                ins = spread_out(0, g_pn[:, 0], half)
            ins.then_inc(diag_ready, 1)
            done(nc.vector.reciprocal(g_p0i[0:TT], g_pn[0:TT, 0]))
            done(nc.vector.tensor_tensor(g_ratio[0:TT], g_pn[0:TT, 1], g_p0i[0:TT], ALU.mult))
            for half in range(2):
                ins = spread_out(1, g_ratio, half)
            ins.then_inc(diag_ready, 1)

            dve.wait_ge(share_mm, 1)
            nc.vector.tensor_tensor(xs[:], xn2[:].rearrange("p (h t) -> p h t", h=2), share_ps, ALU.mult)\
                .then_inc(xs_ready, 1)
            dve.wait_ge(xs_ready, 1)
            nc.vector.tensor_copy(xs_hi[:], xs[:]).then_inc(xshi_ready, 1)
            dve.wait_ge(xshi_ready, 1)
            nc.vector.tensor_tensor(xs_lo[:], xs[:], xs_hi[:].bitcast(F32), ALU.subtract).then_inc(xs_split, 1)
            dve.wait_ge(share_mm, 2)
            nc.vector.tensor_copy(ratio[:], ratio_ps).then_inc(ratio_ready, 1)
            dve.wait_ge(ratio_ready, 1)

            def second_share(n, s):
                dve.wait_ge(ga_ready, n + 1)
                if not (isinstance(n, int) and n < 2):
                    dve.wait_ge(gb_ready, n - 1)
                nc.vector.tensor_tensor(zb[:, s], up_ps[s], ratio[:], ALU.mult).then_inc(zb_ready, 1)

            def hidden_sum(n, s):
                dve.wait_ge(gb_ready, n + 1)
                if not (isinstance(n, int) and n < 2):
                    dve.wait_ge(hid_split, n - 1)
                nc.vector.tensor_tensor(hid[:, s], ga[:, s], gb[:, s], ALU.add).then_inc(hid_ready, 1)

            def low_part(n, s):
                dve.wait_ge(hhi_ready, n + 1)
                nc.vector.tensor_tensor(hid_lo[:, s], hid[:, s], hid_hi[:, s].bitcast(F32), ALU.subtract)\
                    .then_inc(hid_split, 1)

            def step(n, s):
                second_share(n, s)
                if not (isinstance(n, int) and n < 1):
                    hidden_sum(n - 1, 1 - s)
                if not (isinstance(n, int) and n < 2):
                    low_part(n - 2, s)

            for c in range(CF):
                step(c, c % 2)
            with dve.Fori(1, E) as e:
                for c in range(CF):
                    step(e * CF + c, c % 2)
            hidden_sum(NCH - 1, 1)
            low_part(NCH - 2, 0)
            low_part(NCH - 1, 1)

            dve.wait_ge(b2_ready, 1)
            dve.wait_ge(down_done, NCH)
            for half in range(2):
                nc.vector.scalar_tensor_tensor(y[:, half], down_ps[:, half], b2_twice[:, 0:1], h1[:, half],
                                               ALU.add, ALU.add).then_inc(y_ready, 1)

        @block.gpsimd
        def _(pool):
            for m in range(6):
                pool.wait_ge(qkv_in[m], 16)
                nc.gpsimd.tensor_scalar(w_qkv_hi[:, m], w_qkv_sb[:, m], 1.0, 0.0, ALU.mult, ALU.add)\
                    .then_inc(qkv_hi_ready, 1)
                pool.wait_ge(qkv_hi_ready, m + 1)
                nc.gpsimd.tensor_tensor(w_qkv_lo[:, m], w_qkv_sb[:, m], w_qkv_hi[:, m].bitcast(F32), ALU.subtract)\
                    .then_inc(qkv_split, 1)

            def split_w1(e, slot):
                h = 2 * e + slot
                src = w1_sb[:, bass.ds(h * 2 * P, 2 * P)]
                if not (isinstance(h, int) and h < 2):
                    pool.wait_ge(up_done, 2 * h - 2)
                nc.gpsimd.tensor_copy(w1_hi[:, slot], src).then_inc(w1hi_ready, 1)
                pool.wait_ge(w1hi_ready, h + 1)
                pool.nop(nofuse=True)
                nc.gpsimd.tensor_tensor(w1_lo[:, slot], src, w1_hi[:, slot].bitcast(F32), ALU.subtract)\
                    .then_inc(w1_split, 1)

            def split_w2(e, slot):
                h = 2 * e + slot
                src = w2_sb[:, bass.ds(h * 2 * P, 2 * P)]
                if not (isinstance(h, int) and h < 2):
                    pool.wait_ge(down_done, 2 * h - 2)
                nc.gpsimd.tensor_copy(w2_hi[:, slot], src).then_inc(w2hi_ready, 1)
                pool.wait_ge(w2hi_ready, h + 1)
                pool.nop(nofuse=True)
                nc.gpsimd.tensor_tensor(w2_lo[:, slot], src, w2_hi[:, slot].bitcast(F32), ALU.subtract)\
                    .then_inc(w2_split, 1)

            pool.wait_ge(w1_in, 16)
            pool.wait_ge(w2_in, 16)
            for slot in range(2):
                split_w1(0, slot)
            for slot in range(2):
                split_w2(0, slot)
            for slot in range(2):
                split_w1(1, slot)
            with pool.Fori(1, E - 1) as e:
                for slot in range(2):
                    split_w2(e, slot)
                    split_w1(e + 1, slot)
            for slot in range(2):
                split_w2(E - 1, slot)

        @block.sync
        def _(sp):
            sp.dma_start(tok_w_sb[:], tok_w).then_inc(tokw_in, 16)
            for k in range(KP):
                sp.dma_start(patch_sb[:, k], patches[:, k]).then_inc(patch_in[k], 16)
                if k == 0:
                    sp.dma_start(small_sb[:], small).then_inc(small_in, 16)
                if k == 2:
                    sp.dma_start(const_sb[:], consts).then_inc(const_in, 16)
            for m in range(6):
                sp.dma_start(w_qkv_sb[:, m], w_qkv[m]).then_inc(qkv_in[m], 16)
            sp.dma_start(w_out_sb[:], w_out).then_inc(wout_in, 16)
            sp.dma_start(w1_sb[:].rearrange("p (e f) -> p e f", e=E), w1).then_inc(w1_in, 16)
            sp.dma_start(w2_sb[:], w2).then_inc(w2_in, 16)
            for half in range(2):
                sp.wait_ge(y_ready, half + 1)
                sp.dma_start(out[:, half * HT:(half + 1) * HT], y[:, half]).then_inc(stored, 16)
            sp.wait_ge(stored, 32)


def constants(S):
    import numpy as np

    row, col = np.arange(S)[:, None], np.arange(S)[None, :]
    scale = np.float32(64) ** -0.5
    masks = np.zeros((P, 3, S), np.float32)
    for base in (0, 64):
        masks[base:base + S, 0] = np.where(row <= col, scale, 0)
        masks[base:base + S, 1] = np.where(row > col, 0.5, 0)
        masks[base:base + S, 2] = np.where(col <= row, 0, NEG)
    center = np.eye(P) - 1.0 / P
    return np.concatenate([center, np.eye(P), masks.reshape(P, 3 * S)], axis=1).astype(np.float32)


def kernel(**inputs):
    import numpy as np
    import concourse.bacc as bacc
    from concourse.bass_utils import run_bass_kernel_spmd

    x = np.asarray(inputs["x"])
    B, C, H, W = x.shape
    pz = 16
    D = inputs["L0_tok_w"].shape[0]
    hp, wp = H // pz, W // pz
    S = hp * wp
    E, _, DFF = inputs["L0_ffn_W1"].shape
    K = C * pz * pz
    KP = K // P
    HD = inputs["L0_attn_w_q_u"].shape[1]
    dims = dict(B=B, S=S, D=D, HEADS=HD // 64, DH=64, E=E, DFF=DFF, KP=KP)

    def a(name):
        return np.asarray(inputs[name])

    patches = x.reshape(B, C, hp, pz, wp, pz).transpose(1, 3, 5, 0, 2, 4).reshape(KP, P, B * S).transpose(1, 0, 2)
    tok_w = a("L0_tok_w").T.reshape(KP, P, D).transpose(1, 0, 2)
    small = np.concatenate([a("L0_tok_b").reshape(P, 1), a("L0_ffn_b2").T, a("L0_ffn_Wg"),
                            a("L0_ffn_b1").reshape(E * DFF // P, P).T], axis=1)
    arrays = {
        "patches": patches, "tok_w": tok_w, "consts": constants(S), "small": small,
        "w_out": a("L0_attn_w_out").reshape(HD // P, P, D).transpose(1, 0, 2),
        "w1": a("L0_ffn_W1").transpose(1, 0, 2),
        "w2": a("L0_ffn_W2").reshape(E * DFF // P, P, D).transpose(1, 0, 2).reshape(P, E * DFF),
    }
    for n in ("q_u", "k_u", "v_u", "q_c", "k_c", "v_c"):
        arrays[f"w_{n}"] = a(f"L0_attn_w_{n}")
    arrays = {k: np.ascontiguousarray(v) for k, v in arrays.items()}
    nc = bacc.Bacc("TRN2", target_bir_lowering=False, num_devices=1)
    ap = {k: nc.dram_tensor(k, v.shape, mybir.dt.from_np(v.dtype), kind="ExternalInput").ap() for k, v in arrays.items()}
    out = nc.dram_tensor("out", (D, B * S), F32, kind="ExternalOutput").ap()
    vit_layer(nc, ap["patches"], ap["tok_w"], ap["consts"], ap["small"],
              [ap[f"w_{n}"] for n in ("q_u", "k_u", "v_u", "q_c", "k_c", "v_c")],
              ap["w_out"], ap["w1"], ap["w2"], out, dims)
    r = run_bass_kernel_spmd(nc, [arrays], core_ids=[0])
    return r.results[0]["out"].T.reshape(B, S, D)
```

```python
from contextlib import ExitStack

import concourse.bass as bass
from concourse import mybir

P = 128
F32 = mybir.dt.float32
F32R = mybir.dt.float32r
ALU = mybir.AluOpType
ACT = mybir.ActivationFunctionType
AX_X = mybir.AxisListType.X
EPS = 1e-5
NEG = -1e30

QU, KU, VU, QC, KC, VC = range(6)


def vit_layer(nc, patches, tok_w, consts, small, w_qkv, w_out, w1, w2, out, dims):
    B, S, D, HEADS, DH, E, DFF, KP = (dims[k] for k in ("B", "S", "D", "HEADS", "DH", "E", "DFF", "KP"))
    T = B * S
    HT = T // 2
    CH = HEADS * DH // P
    CF = DFF // P
    NB = 4
    NG = B // NB
    GT = NB * S
    ROWS = P
    BLK = CH * (NB // 2)
    WIDE = BLK * S
    TT = 96
    NT = T // TT
    NCH = E * CF
    SCALE = float(DH) ** -0.5
    assert D == P and DH == 64 and S <= 64 and WIDE <= 512 and HT <= 512 and NT * TT == T and CF == 4

    with ExitStack() as ctx:
        def sb(name, shape, dt=F32):
            return ctx.enter_context(nc.sbuf_tensor(name, shape, dt))

        def sem(name):
            return ctx.enter_context(nc.semaphore(name))

        ps = ctx.enter_context(nc.psum_tensor("ps", [P, 8, 512], F32))

        patch_sb = sb("patch_sb", [P, KP, T])
        tok_w_sb = sb("tok_w_sb", [P, KP, D])
        const_sb = sb("const_sb", [P, 2 * P + 3 * S])
        small_sb = sb("small_sb", [P, 1 + 2 * E + E * CF])
        center = const_sb[:, 0:P]
        ident = const_sb[:, P:2 * P]
        tok_b = small_sb[:, 0:1]
        b2_sb = small_sb[:, 1:1 + E]
        w_gate = small_sb[:, 1 + E:1 + 2 * E]
        b1_sb = small_sb[:, 1 + 2 * E:1 + 2 * E + E * CF]
        w_qkv_sb = sb("w_qkv_sb", [P, 6, CH * P])
        w_qkv_hi = sb("w_qkv_hi", [P, 6, CH * P], F32R)
        w_qkv_lo = sb("w_qkv_lo", [P, 6, CH * P], F32R)
        w_out_sb = sb("w_out_sb", [P, CH, D])
        w1_sb = sb("w1_sb", [P, E * DFF])
        w2_sb = sb("w2_sb", [P, E * DFF])
        mean_w = sb("mean_w", [P, P])
        ones = sb("ones", [P, P])
        eps = sb("eps", [P, 1])
        masks = sb("masks", [P, 3, BLK, S])
        gate_mask, look_mask, causal_mask = (masks[0:ROWS, k].rearrange("p n s -> p (n s)") for k in range(3))

        h0 = sb("h0", [P, 2, HT])
        h1 = sb("h1", [P, 2, HT])
        sq = sb("sq", [P, 2, HT])
        xc = sb("xc", [P, 2, HT])
        sd = sb("sd", [P, NT])
        rstd = sb("rstd", [P, NT])
        xn = sb("xn", [P, T])

        x_hi = sb("x_hi", [P, B, 64], F32R)
        x_lo = sb("x_lo", [P, B, 64], F32R)
        qk = sb("qk", [P, 5, CH, T])
        v_sb = sb("v_sb", [P, B // 2, CH * P])
        gate = sb("gate", [P, 2, WIDE])
        look = sb("look", [P, 2, WIDE])
        sc_m = sb("sc_m", [P, 2, WIDE])
        soft = sb("soft", [P, 2, 2, WIDE])
        prob_t = sb("prob_t", [P, 2, BLK, 2, S])
        row_max = sb("row_max", [P, 2 * BLK])
        row_sum = sb("row_sum", [P, 2 * BLK])
        row_inv = sb("row_inv", [P, 2 * BLK])
        o_t = sb("o_t", [P, CH, T])

        g_max = sb("g_max", [P, NT])
        g_shift = sb("g_shift", [P, NT, E])
        g_exp = sb("g_exp", [P, NT, E])
        g_sum = sb("g_sum", [P, NT])
        g_inv = sb("g_inv", [P, NT])
        g_prob = sb("g_prob", [P, NT, E])
        g_top = sb("g_top", [P, NT, 8])
        g_two = sb("g_two", [P, NT])
        g_twoi = sb("g_twoi", [P, NT])
        g_pn = sb("g_pn", [P, 2, NT])
        g_p0i = sb("g_p0i", [P, NT])
        g_ratio = sb("g_ratio", [P, NT])
        diag = sb("diag", [P, 2, NT, TT])
        late = qk[:].rearrange("p a b t -> p (a b) t")
        xn2 = late[:, 0]
        xs, ratio = (late[:, k].rearrange("p (h t) -> p h t", h=2) for k in (1, 2))

        def halves(tile, slots, start=0):
            flat = tile[:].rearrange("p a b -> p (a b)")[:, start:start + slots * T]
            return flat.rearrange("p (s h t) -> p s h t", s=slots, h=2)

        ga, gb = halves(patch_sb, 4), halves(patch_sb, 2, 4 * T)
        zb, hid = halves(w_qkv_sb, 2), halves(w_qkv_sb, 2, 2 * T)

        def split_parts(tile):
            w = tile[:].rearrange("p a b -> p (a b)")[:, T:T + 4 * P]
            return halves(tile, 1)[:, 0], w.rearrange("p (s n) -> p s n", s=2)

        xs_hi, w1_hi = split_parts(w_qkv_hi)
        xs_lo, w1_lo = split_parts(w_qkv_lo)
        w2_ring = sb("w2_ring", [P, 2, 2 * P])
        b2_sum = sb("b2_sum", [P, 1])
        b2_twice = sb("b2_twice", [P, 1])
        y = xs

        tokw_in, const_in, small_in = sem("tokw_in"), sem("const_in"), sem("small_in")
        patch_in = [sem(f"patch_in{k}") for k in range(KP)]
        qkv_in = [sem(f"qkv_in{k}") for k in range(6)]
        wout_in, w1_in, w2_in = sem("wout_in"), sem("w1_in"), sem("w2_in")
        stored = sem("stored")
        psum_clear, fills, masks_ready, xpads_ready = sem("psum_clear"), sem("fills"), sem("masks_ready"), sem("xpads_ready")
        qkv_hi_ready, qkv_split = sem("qkv_hi_ready"), sem("qkv_split")
        emb_done, res_ready = sem("emb_done"), sem("res_ready")
        cen_done, xc_ready, sq_ready, var_done, sd_ready, rstd_ready, ndiag_ready, norm_mm, xn_ready = (
            sem("cen_done"), sem("xc_ready"), sem("sq_ready"), sem("var_done"), sem("sd_ready"), sem("rstd_ready"),
            sem("ndiag_ready"), sem("norm_mm"), sem("xn_ready"))
        xhi_ready, x_split = sem("xhi_ready"), sem("x_split")
        part_done = sem("part_done")
        part_taken = [sem(f"part_taken{b}") for b in range(4)]
        look_done, sc_done, gate_done, su_done = sem("look_done"), sem("sc_done"), sem("gate_done"), sem("su_done")
        lookt_ready, look_ready, scm_ready, gate_ready = (
            sem("lookt_ready"), sem("look_ready"), sem("scm_ready"), sem("gate_ready"))
        sut_ready, su_ready, logit_ready, max_ready, shift_ready, exp_ready, sum_ready, inv_ready, prob_ready = (
            sem("sut_ready"), sem("su_ready"), sem("logit_ready"), sem("max_ready"), sem("shift_ready"),
            sem("exp_ready"), sem("sum_ready"), sem("inv_ready"), sem("prob_ready"))
        pt_done, pt_ready, pv_done, o_ready = sem("pt_done"), sem("pt_ready"), sem("pv_done"), sem("o_ready")
        proj_done = sem("proj_done")
        route_mm, route_step, route_exp, diag_ready, share_mm = (
            sem("route_mm"), sem("route_step"), sem("route_exp"), sem("diag_ready"), sem("share_mm"))
        xs_ready, xshi_ready, xs_split, ratio_ready = sem("xs_ready"), sem("xshi_ready"), sem("xs_split"), sem("ratio_ready")
        w1hi_ready, w1_split, w2_ready = sem("w1hi_ready"), sem("w1_split"), sem("w2_ready")
        up_done, down_done, zb_ready, ga_ready, gb_ready, hid_ready = (
            sem("up_done"), sem("down_done"), sem("zb_ready"), sem("ga_ready"), sem("gb_ready"),
            sem("hid_ready"))
        b2s_ready, b2_ready, y_ready = sem("b2s_ready"), sem("b2_ready"), sem("y_ready")

        def pair(b, n):
            return ps[:, b:b + 2, 0:n]

        emb_ps, cen_ps, norm_ps = pair(0, HT), pair(2, HT), pair(6, HT)
        var_ps = ps[0:TT, 4:6, 0:NT // 2]
        gate_ps, look_ps, sc_ps = pair(2, WIDE), pair(4, WIDE), pair(6, WIDE)
        su_ps, pt_ps, o_ps = gate_ps, look_ps, sc_ps
        attn_ps = pair(0, HT)
        route_ps = ps[0:TT, 4, 0:NT * E].rearrange("p (n e) -> p n e", n=NT)
        share_ps, ratio_ps = pair(6, HT), pair(0, HT)
        down_ps, up_ps = pair(0, HT), (pair(2, HT), pair(4, HT))

        NQK = 5 * CH
        EARLY = 3 * CH

        def part_qk(h, k):
            return h * NQK + k + (2 if h == 1 and k >= EARLY else 0)

        def part_v(pair):
            return NQK + EARLY + pair if pair < 2 else 2 * NQK + pair

        def bank(part):
            return part % 4 if part < NQK else part % 2

        def by_vector(part):
            return part < NQK and part % 2 == 1

        def taken(eng, part):
            before = sum(bank(k) == bank(part) for k in range(part))
            eng.wait_ge(part_taken[bank(part)], before + 1)

        def bank_before(part):
            return max((k for k in range(part) if bank(k) == bank(part)), default=None)

        def split_mm(pe, dst, w, w_lo, x, x_lo, first=True, last=True):
            pe.matmul(dst, w, x, start=first, stop=False)
            pe.matmul(dst, w_lo, x, start=False, stop=False)
            return pe.matmul(dst, w, x_lo, start=False, stop=last)

        block = ctx.enter_context(nc.Block())

        @block.tensor
        def _(pe):
            def layer_norm(k):
                res = h0 if k == 0 else h1
                if k == 0:
                    pe.wait_ge(const_in, 16)
                    pe.wait_ge(fills, 2)
                for half in range(2):
                    pe.wait_ge(res_ready, 2 * k + half + 1)
                    pe.matmul(cen_ps[:, half], center, res[:, half], start=True, stop=True).then_inc(cen_done, 1)
                for half in range(2):
                    pe.wait_ge(sq_ready, 2 * k + half + 1)
                    for n in range(NT // 2):
                        mm = pe.matmul(var_ps[:, half, n:n + 1], sq[:, half, n * TT:(n + 1) * TT], mean_w[:, 0:1],
                                       start=True, stop=True)
                    mm.then_inc(var_done, 1)
                for half in range(2):
                    pe.wait_ge(ndiag_ready, 2 * k + half + 1)
                    spread(norm_ps, 0, half).then_inc(norm_mm, 1)

            def spread(dst, k, half):
                tiles = slice(half * NT // 2, (half + 1) * NT // 2)
                return pe.matmul(dst[:, half], ones[0:TT, :], diag[0:TT, k, tiles].rearrange("p n t -> p (n t)"),
                                 start=True, stop=True)

            pe.wait_ge(tokw_in, 16)
            for k in range(KP):
                pe.wait_ge(patch_in[k], 16)
                for half in range(2):
                    mm = pe.matmul(emb_ps[:, half], tok_w_sb[:, k], patch_sb[:, k, half * HT:(half + 1) * HT],
                                   start=(k == 0), stop=(k == KP - 1))
                    if k == KP - 1:
                        mm.then_inc(emb_done, 1)
            pe.wait_ge(psum_clear, 2)
            layer_norm(0)

            def project_qk(h, first, last):
                pe.wait_ge(x_split, h + 1)
                for k in range(first, last):
                    m, c = divmod(k, CH)
                    part = part_qk(h, k)
                    if h == 0 and c == 0:
                        pe.wait_ge(qkv_split, m + 1)
                    if bank_before(part) is not None:
                        taken(pe, bank_before(part))
                    ch, two = slice(c * P, (c + 1) * P), slice(h * B // 2, (h + 1) * B // 2)
                    split_mm(pe, ps[:, bank(part), 0:HT], w_qkv_hi[:, m, ch], w_qkv_lo[:, m, ch],
                             x_hi[:, two, 0:S], x_lo[:, two, 0:S]).then_inc(part_done, 1)

            def project_v(pair):
                part = part_v(pair)
                pe.wait_ge(qkv_split, 6)
                taken(pe, bank_before(part))
                two = slice(2 * pair, 2 * pair + 2)
                split_mm(pe, ps[:, bank(part), :], x_hi[:, two].rearrange("p b s -> p (b s)"),
                         x_lo[:, two].rearrange("p b s -> p (b s)"),
                         w_qkv_hi[:, VC], w_qkv_lo[:, VC]).then_inc(part_done, 1)

            def by_head(g, dst, a, b):
                for blk in range(BLK):
                    c, q = divmod(blk, NB // 2)
                    for hp in range(2):
                        for bp in range(2):
                            at = g * GT + (2 * q + bp) * S
                            rows = slice(64 * hp, 64 * hp + 64)
                            mm = pe.matmul(dst[64 * bp:64 * bp + S, hp, blk * S:(blk + 1) * S],
                                           qk[rows, a, c, at:at + S], qk[rows, b, c, at:at + S], start=True, stop=True)
                return mm

            def projected(g, *projections):
                for m in projections:
                    for c in range(CH):
                        taken(pe, part_qk(g // 2, m * CH + c))

            def look_scores(g):
                projected(g, QU, KU)
                if g == 1:
                    pe.wait_ge(lookt_ready, 1)
                if g >= 2:
                    pe.wait_ge(pt_ready, 2 * (g - 1))
                by_head(g, look_ps, KU, QU).then_inc(look_done, 1)

            def gate_scores(g):
                projected(g, VU, QC)
                if g == 0:
                    projected(g, KC)
                else:
                    pe.wait_ge(su_ready, g)
                by_head(g, gate_ps, VU, QC).then_inc(gate_done, 1)

            def causal_scores(g):
                projected(g, QC, KC)
                if g == 1:
                    pe.wait_ge(scm_ready, 1)
                if g >= 2:
                    pe.wait_ge(o_ready, 2 * (g - 1))
                by_head(g, sc_ps, QC, KC).then_inc(sc_done, 1)

            def gate_sums(g):
                pe.wait_ge(look_ready, g + 1)
                pe.wait_ge(gate_ready, g + 1)
                for hp in range(2):
                    for blk in range(BLK):
                        for bp in range(2):
                            rows, cols = slice(64 * bp, 64 * bp + 64), slice(blk * S, (blk + 1) * S)
                            mm = pe.matmul(su_ps[64 * bp:64 * bp + S, hp, cols], gate[rows, hp, cols],
                                           look[rows, hp, cols], start=True, stop=True)
                mm.then_inc(su_done, 1)

            def transpose_probs(g):
                if g < NG - 1:
                    pe.wait_ge(lookt_ready, g + 2)
                else:
                    pe.wait_ge(pt_ready, 2 * g)
                pe.wait_ge(prob_ready, g + 1)
                for hp in range(2):
                    for blk in range(BLK):
                        for bp in range(2):
                            rows, cols = slice(64 * bp, 64 * bp + 64), slice(blk * S, (blk + 1) * S)
                            mm = pe.matmul(pt_ps[64 * bp:64 * bp + S, hp, cols], soft[rows, g % 2, hp, cols],
                                           ident[rows, 64 * bp:64 * bp + S], start=True, stop=True)
                    mm.then_inc(pt_done, 1)

            def weighted_values(g):
                if g < NG - 1:
                    pe.wait_ge(scm_ready, g + 2)
                else:
                    pe.wait_ge(o_ready, 2 * g)
                for q in range(2):
                    taken(pe, part_v(2 * g + q))
                for hp in range(2):
                    pe.wait_ge(pt_ready, 2 * g + hp + 1)
                    for blk in range(BLK):
                        c, q = divmod(blk, NB // 2)
                        head = slice((2 * c + hp) * 64, (2 * c + hp + 1) * 64)
                        mm = pe.matmul(o_ps[64 * hp:64 * hp + 64, q, c * 2 * S:(c + 1) * 2 * S],
                                       v_sb[:, 2 * g + q, head], prob_t[:, hp, blk], start=True, stop=True)
                mm.then_inc(pv_done, 1)

            def project_out(half):
                pe.wait_ge(o_ready, 4 * (half + 1))
                pe.wait_ge(wout_in, 16)
                taken(pe, part_v(B // 2 - 2 + half))
                for c in range(CH):
                    mm = pe.matmul(attn_ps[:, half], w_out_sb[:, c], o_t[:, c, half * HT:(half + 1) * HT],
                                   start=(c == 0), stop=(c == CH - 1))
                mm.then_inc(proj_done, 1)

            project_qk(0, 0, NQK)
            look_scores(0)
            project_qk(1, 0, 1)
            gate_scores(0)
            project_qk(1, 1, 2)
            causal_scores(0)
            project_qk(1, 2, 4)
            gate_sums(0)
            project_qk(1, 4, 5)
            look_scores(1)
            project_qk(1, 5, 6)
            gate_scores(1)
            project_qk(1, 6, 7)
            causal_scores(1)
            project_qk(1, 7, 9)
            gate_sums(1)
            project_qk(1, 9, 12)
            transpose_probs(0)
            project_v(0)
            project_v(1)
            weighted_values(0)
            project_qk(1, 12, 14)
            look_scores(2)
            project_qk(1, 14, 17)
            gate_scores(2)
            project_qk(1, 17, 20)
            causal_scores(2)
            project_v(2)
            gate_sums(2)
            project_v(3)
            transpose_probs(1)
            weighted_values(1)
            project_v(4)
            look_scores(3)
            gate_scores(3)
            project_v(5)
            causal_scores(3)
            gate_sums(3)
            project_v(6)
            transpose_probs(2)
            weighted_values(2)
            project_v(7)
            project_out(0)
            transpose_probs(3)
            weighted_values(3)
            project_out(1)

            layer_norm(1)

            pe.wait_ge(xn_ready, 4)
            for n in range(NT):
                mm = pe.matmul(route_ps[:, n], xn2[:, n * TT:(n + 1) * TT], w_gate, start=True, stop=True)
            mm.then_inc(route_mm, 1)
            for k, dst in enumerate((share_ps, ratio_ps)):
                pe.wait_ge(diag_ready, k + 1)
                for half in range(2):
                    mm = spread(dst, k, half)
                mm.then_inc(share_mm, 1)

            def up(e, c):
                n = e * CF + c
                slot, at = c // 2, slice((c % 2) * P, (c % 2 + 1) * P)
                pe.wait_ge(w1_split, 2 * e + slot + 1)
                if not (isinstance(n, int) and n < 2):
                    pe.wait_ge(zb_ready, n - 1)
                for half in range(2):
                    mm = split_mm(pe, up_ps[c % 2][:, half], w1_hi[:, slot, at], w1_lo[:, slot, at],
                                  xs_hi[:, half], xs_lo[:, half])
                mm.then_inc(up_done, 1)

            def down(e, c):
                n = e * CF + c
                slot, at = c // 2, slice((c % 2) * P, (c % 2 + 1) * P)
                first, last = isinstance(n, int) and n == 0, isinstance(n, int) and n == NCH - 1
                pe.wait_ge(w2_ready, 2 * e + slot + 1)
                pe.wait_ge(hid_ready, n + 1)
                for half in range(2):
                    mm = pe.matmul(down_ps[:, half], w2_ring[:, slot, at], hid[:, c % 2, half], start=first, stop=last)
                mm.then_inc(down_done, 1)

            pe.wait_ge(xs_split, 1)
            for c in range(CF):
                up(0, c)
            pe.wait_ge(ratio_ready, 1)
            for c in range(CF):
                up(1, c)
                down(0, c)
            with pe.Fori(1, E - 1) as e:
                for c in range(CF):
                    up(e + 1, c)
                    down(e, c)
            for c in range(CF):
                down(E - 1, c)

        @block.scalar
        def _(act):
            nc.scalar.preload_act_table(ACT.Sqrt)
            act.wait_ge(small_in, 16)
            for half in range(2):
                act.wait_ge(emb_done, half + 1)
                nc.scalar.activation(h0[:, half], emb_ps[:, half], ACT.Identity, bias=tok_b).then_inc(res_ready, 1)

            def layer_norm(k):
                for half in range(2):
                    act.wait_ge(cen_done, 2 * k + half + 1)
                    nc.scalar.copy(xc[:, half], cen_ps[:, half]).then_inc(xc_ready, 1)
                act.wait_ge(var_done, 2 * k + 2)
                nc.scalar.activation(sd[0:TT, :].rearrange("p (h n) -> p h n", h=2), var_ps, ACT.Sqrt,
                                     bias=eps[0:TT]).then_inc(sd_ready, 1)

            act.wait_ge(fills, 3)
            layer_norm(0)
            nc.scalar.preload_act_table(ACT.Tanh)

            def take_qk(h, first, last):
                for k in range(first, last):
                    m, c = divmod(k, CH)
                    part = part_qk(h, k)
                    if by_vector(part):
                        continue
                    act.wait_ge(part_done, part + 1)
                    nc.scalar.copy(qk[:, m, c, h * HT:(h + 1) * HT], ps[:, bank(part), 0:HT])\
                        .then_inc(part_taken[bank(part)], 1)

            def take_v(pair):
                act.wait_ge(part_done, part_v(pair) + 1)
                nc.scalar.copy(v_sb[:, pair], ps[:, bank(part_v(pair)), :]).then_inc(part_taken[pair % 2], 1)

            def lookahead(g):
                act.wait_ge(look_done, g + 1)
                if g >= 1:
                    act.wait_ge(su_done, g)
                nc.scalar.activation(look[0:ROWS], look_ps[0:ROWS], ACT.Tanh, scale=SCALE / 2)\
                    .then_inc(lookt_ready, 1)

            def gate_tanh(g):
                act.wait_ge(su_done, g + 1)
                if g >= 2:
                    act.wait_ge(pt_done, 2 * (g - 1))
                nc.scalar.activation(soft[0:ROWS, g % 2], su_ps[0:ROWS], ACT.Tanh, scale=0.5).then_inc(sut_ready, 1)

            def exponent(g):
                act.wait_ge(shift_ready, g + 1)
                nc.scalar.activation(soft[0:ROWS, g % 2], soft[0:ROWS, g % 2], ACT.Exp, scale=SCALE).then_inc(exp_ready, 1)

            def take_probs(g):
                for hp in range(2):
                    act.wait_ge(pt_done, 2 * g + hp + 1)
                    if g == 0:
                        act.wait_ge(fills, 4)
                    if g >= 1:
                        act.wait_ge(pv_done, g)
                    for bp in range(2):
                        rows = slice(64 * bp, 64 * bp + S)
                        ins = nc.scalar.copy(prob_t[rows, hp, :, bp], pt_ps[rows, hp].rearrange("p (n s) -> p n s", s=S))
                    ins.then_inc(pt_ready, 1)

            def take_o(g):
                act.wait_ge(pv_done, g + 1)
                for q in range(2):
                    at = o_t[:].rearrange("p c (g q w) -> p c g q w", g=NG, q=2)
                    nc.scalar.copy(at[:, :, g, q], o_ps[:, q].rearrange("p (c w) -> p c w", c=CH)).then_inc(o_ready, 1)

            take_qk(0, 0, NQK)
            lookahead(0)
            take_qk(1, 0, 4)
            gate_tanh(0)
            take_qk(1, 4, 5)
            lookahead(1)
            take_qk(1, 5, 7)
            exponent(0)
            take_qk(1, 7, 9)
            gate_tanh(1)
            take_qk(1, 9, 12)
            take_probs(0)
            take_v(0)
            take_v(1)
            exponent(1)
            take_o(0)
            take_qk(1, 12, 14)
            lookahead(2)
            take_qk(1, 14, 20)
            take_v(2)
            gate_tanh(2)
            take_v(3)
            take_probs(1)
            take_o(1)
            take_v(4)
            exponent(2)
            lookahead(3)
            take_v(5)
            gate_tanh(3)
            take_v(6)
            take_probs(2)
            take_o(2)
            take_v(7)
            exponent(3)
            take_probs(NG - 1)
            take_o(NG - 1)

            nc.scalar.preload_act_table(ACT.Sqrt)
            layer_norm(1)
            nc.scalar.preload_act_table(ACT.Exp)
            act.wait_ge(route_step, 2)
            nc.scalar.activation(g_exp[0:TT], g_shift[0:TT], ACT.Exp).then_inc(route_exp, 1)
            nc.scalar.preload_act_table(ACT.Gelu)

            def gelu_first(n, c):
                s = c % 2
                act.wait_ge(up_done, n + 1)
                if not (isinstance(n, int) and n < 4):
                    act.wait_ge(hid_ready, n - 3)
                act.nop(nofuse=True)
                nc.scalar.activation(ga[:, c], up_ps[s], ACT.Gelu, bias=b1_sb[:, bass.ds(n, 1)]).then_inc(ga_ready, 1)

            def gelu_second(n, s):
                act.wait_ge(zb_ready, n + 1)
                if not (isinstance(n, int) and n < 2):
                    act.wait_ge(hid_ready, n - 1)
                act.nop(nofuse=True)
                nc.scalar.activation(gb[:, s], zb[:, s], ACT.Gelu, bias=b1_sb[:, bass.ds(n, 1)]).then_inc(gb_ready, 1)

            def step(n, c):
                s = c % 2
                gelu_first(n, c)
                if not (isinstance(n, int) and n < 1):
                    gelu_second(n - 1, 1 - s)

            for c in range(CF):
                step(c, c)
            with act.Fori(1, E) as e:
                for c in range(CF):
                    step(e * CF + c, c)
            gelu_second(NCH - 1, 1)

        @block.vector
        def _(dve):
            nc.vector.memset(mean_w[:], 1.0 / D).then_inc(fills, 1)
            nc.vector.memset(ones[:], 1.0).then_inc(fills, 1)
            nc.vector.memset(eps[:], EPS).then_inc(fills, 1)
            nc.vector.memset(x_hi[:, :, S:].bitcast(F32), 0.0).then_inc(xpads_ready, 1)
            nc.vector.memset(x_lo[:, :, S:].bitcast(F32), 0.0).then_inc(xpads_ready, 1)
            for above in (32, 96):
                nc.vector.memset(ps[above:above + 32, 2:8, 0:WIDE], 0.0).then_inc(psum_clear, 1)
            nc.vector.memset(prob_t[:], 0.0).then_inc(fills, 1)
            dve.wait_ge(const_in, 16)
            nc.vector.tensor_copy(
                masks[:], const_sb[:, 2 * P:].rearrange("p (k o s) -> p k o s", k=3, o=1).broadcast_to([P, 3, BLK, S]))\
                .then_inc(masks_ready, 1)
            dve.wait_ge(small_in, 16)
            nc.vector.reduce_sum(b2_sum[:], b2_sb, AX_X).then_inc(b2s_ready, 1)
            dve.wait_ge(b2s_ready, 1)
            nc.vector.tensor_scalar(b2_twice[:], b2_sum[:], 2.0, None, ALU.mult).then_inc(b2_ready, 1)

            def layer_norm(k, dst):
                for half in range(2):
                    dve.wait_ge(xc_ready, 2 * k + half + 1)
                    nc.vector.tensor_tensor(sq[:, half], xc[:, half], xc[:, half], ALU.mult).then_inc(sq_ready, 1)
                dve.wait_ge(sd_ready, k + 1)
                nc.vector.reciprocal(rstd[0:TT, :], sd[0:TT, :]).then_inc(rstd_ready, 1)
                dve.wait_ge(rstd_ready, k + 1)
                for half in range(2):
                    spread_out(0, rstd, half).then_inc(ndiag_ready, 1)
                for half in range(2):
                    dve.wait_ge(norm_mm, 2 * k + half + 1)
                    nc.vector.tensor_tensor(dst[:, half * HT:(half + 1) * HT], xc[:, half], norm_ps[:, half],
                                            ALU.mult).then_inc(xn_ready, 1)
                    if k == 0:
                        split_x(half)

            def spread_out(k, by_token, half):
                tiles = slice(half * NT // 2, (half + 1) * NT // 2)
                n = NT // 2
                return nc.vector.tensor_tensor(
                    diag[0:TT, k, tiles],
                    ident[0:TT, 0:TT].rearrange("p (o t) -> p o t", o=1).broadcast_to([TT, n, TT]),
                    by_token[0:TT, tiles].rearrange("p (n o) -> p n o", o=1).broadcast_to([TT, n, TT]), ALU.mult)

            def split_x(h):
                images = slice(h * B // 2, (h + 1) * B // 2)
                x = xn[:, h * HT:(h + 1) * HT].rearrange("p (b s) -> p b s", s=S)
                dve.wait_ge(xn_ready, h + 1)
                nc.vector.tensor_copy(x_hi[:, images, 0:S], x).then_inc(xhi_ready, 1)
                dve.wait_ge(xhi_ready, h + 1)
                nc.vector.tensor_tensor(x_lo[:, images, 0:S], x, x_hi[:, images, 0:S].bitcast(F32), ALU.subtract)\
                    .then_inc(x_split, 1)

            layer_norm(0, xn)

            def take_qk():
                for part in filter(by_vector, range(NQK)):
                    m, c = divmod(part, CH)
                    dve.wait_ge(part_done, part + 1)
                    nc.vector.tensor_copy(qk[:, m, c, 0:HT], ps[:, bank(part), 0:HT])\
                        .then_inc(part_taken[bank(part)], 1)

            def over(mask):
                return mask.rearrange("p (o w) -> p o w", o=1).broadcast_to([ROWS, 2, WIDE])

            def wide(rows):
                return rows[0:ROWS].rearrange("p (n o) -> p n o", o=1).broadcast_to([ROWS, 2 * BLK, S])

            def soft_blocks(g):
                return soft[0:ROWS, g % 2].rearrange("p h (n s) -> p (h n) s", s=S)

            def mask_look(g):
                dve.wait_ge(lookt_ready, g + 1)
                nc.vector.scalar_tensor_tensor(look[0:ROWS], look[0:ROWS], 1.0, over(look_mask), ALU.add, ALU.mult)\
                    .then_inc(look_ready, 1)

            def mask_scores(g):
                dve.wait_ge(sc_done, g + 1)
                if g >= 1:
                    dve.wait_ge(logit_ready, g)
                nc.vector.tensor_tensor(sc_m[0:ROWS], sc_ps[0:ROWS], over(causal_mask), ALU.add)\
                    .then_inc(scm_ready, 1)

            def mask_gate(g):
                dve.wait_ge(gate_done, g + 1)
                if g >= 1:
                    dve.wait_ge(su_done, g)
                nc.vector.tensor_tensor(gate[0:ROWS], gate_ps[0:ROWS], over(gate_mask), ALU.mult)\
                    .then_inc(gate_ready, 1)

            def logits(g):
                dve.wait_ge(sut_ready, g + 1)
                nc.vector.scalar_tensor_tensor(soft[0:ROWS, g % 2], soft[0:ROWS, g % 2], 1.0, su_ps[0:ROWS], ALU.add, ALU.mult)\
                    .then_inc(su_ready, 1)
                dve.wait_ge(su_ready, g + 1)
                dve.wait_ge(scm_ready, g + 1)
                nc.vector.scalar_tensor_tensor(soft[0:ROWS, g % 2], soft[0:ROWS, g % 2], -0.5 / SCALE, sc_m[0:ROWS],
                                               ALU.mult, ALU.add).then_inc(logit_ready, 1)
                dve.wait_ge(logit_ready, g + 1)
                nc.vector.tensor_reduce(row_max[0:ROWS], soft_blocks(g), AX_X, ALU.max).then_inc(max_ready, 1)
                dve.wait_ge(max_ready, g + 1)
                nc.vector.tensor_tensor(soft_blocks(g), soft_blocks(g), wide(row_max), ALU.subtract)\
                    .then_inc(shift_ready, 1)

            def normalise(g):
                dve.wait_ge(exp_ready, g + 1)
                nc.vector.tensor_reduce(row_sum[0:ROWS], soft_blocks(g), AX_X, ALU.add).then_inc(sum_ready, 1)
                dve.wait_ge(sum_ready, g + 1)
                nc.vector.reciprocal(row_inv[0:ROWS], row_sum[0:ROWS]).then_inc(inv_ready, 1)
                dve.wait_ge(inv_ready, g + 1)
                nc.vector.tensor_tensor(soft_blocks(g), soft_blocks(g), wide(row_inv), ALU.mult).then_inc(prob_ready, 1)

            take_qk()
            dve.wait_ge(masks_ready, 1)
            mask_look(0)
            mask_gate(0)
            mask_scores(0)
            for g in range(NG):
                logits(g)
                if g < NG - 1:
                    mask_look(g + 1)
                    mask_gate(g + 1)
                normalise(g)
                if g < NG - 1:
                    mask_scores(g + 1)

            for half in range(2):
                dve.wait_ge(proj_done, half + 1)
                nc.vector.tensor_tensor(h1[:, half], attn_ps[:, half], h0[:, half], ALU.add).then_inc(res_ready, 1)
            layer_norm(1, xn2)

            steps = 0

            def done(ins):
                nonlocal steps
                steps += 1
                ins.then_inc(route_step, 1)
                dve.wait_ge(route_step, steps)

            def over_experts(v):
                return v[0:TT].rearrange("p (n o) -> p n o", o=1).broadcast_to([TT, NT, E])

            dve.wait_ge(route_mm, 1)
            done(nc.vector.tensor_reduce(g_max[0:TT], route_ps, AX_X, ALU.max))
            done(nc.vector.tensor_tensor(g_shift[0:TT], route_ps, over_experts(g_max), ALU.subtract))
            dve.wait_ge(route_exp, 1)
            done(nc.vector.tensor_reduce(g_sum[0:TT], g_exp[0:TT], AX_X, ALU.add))
            done(nc.vector.reciprocal(g_inv[0:TT], g_sum[0:TT]))
            done(nc.vector.tensor_tensor(g_prob[0:TT], g_exp[0:TT], over_experts(g_inv), ALU.mult))
            for n in range(NT - 1):
                nc.vector.max(g_top[0:TT, n], g_prob[0:TT, n])
            done(nc.vector.max(g_top[0:TT, NT - 1], g_prob[0:TT, NT - 1]))
            done(nc.vector.tensor_tensor(g_two[0:TT], g_top[0:TT, :, 0], g_top[0:TT, :, 1], ALU.add))
            done(nc.vector.reciprocal(g_twoi[0:TT], g_two[0:TT]))
            for k in range(2):
                done(nc.vector.tensor_tensor(g_pn[0:TT, k], g_top[0:TT, :, k], g_twoi[0:TT], ALU.mult))
            for half in range(2):
                ins = spread_out(0, g_pn[:, 0], half)
            ins.then_inc(diag_ready, 1)
            done(nc.vector.reciprocal(g_p0i[0:TT], g_pn[0:TT, 0]))
            done(nc.vector.tensor_tensor(g_ratio[0:TT], g_pn[0:TT, 1], g_p0i[0:TT], ALU.mult))
            for half in range(2):
                ins = spread_out(1, g_ratio, half)
            ins.then_inc(diag_ready, 1)

            dve.wait_ge(share_mm, 1)
            nc.vector.tensor_tensor(xs, xn2.rearrange("p (h t) -> p h t", h=2), share_ps, ALU.mult)\
                .then_inc(xs_ready, 1)
            dve.wait_ge(xs_ready, 1)
            nc.vector.tensor_copy(xs_hi[:], xs).then_inc(xshi_ready, 1)
            dve.wait_ge(xshi_ready, 1)
            nc.vector.tensor_tensor(xs_lo[:], xs, xs_hi[:].bitcast(F32), ALU.subtract).then_inc(xs_split, 1)
            dve.wait_ge(share_mm, 2)
            nc.vector.tensor_copy(ratio, ratio_ps).then_inc(ratio_ready, 1)
            dve.wait_ge(ratio_ready, 1)

            def second_share(n, s):
                dve.wait_ge(ga_ready, n + 1)
                if not (isinstance(n, int) and n < 2):
                    dve.wait_ge(gb_ready, n - 1)
                nc.vector.tensor_tensor(zb[:, s], up_ps[s], ratio, ALU.mult).then_inc(zb_ready, 1)

            def hidden_sum(n, c):
                s = c % 2
                dve.wait_ge(gb_ready, n + 1)
                if not (isinstance(n, int) and n < 2):
                    dve.wait_ge(down_done, n - 1)
                nc.vector.tensor_tensor(hid[:, s], ga[:, c], gb[:, s], ALU.add).then_inc(hid_ready, 1)

            def step(n, c):
                s = c % 2
                second_share(n, s)
                if not (isinstance(n, int) and n < 1):
                    hidden_sum(n - 1, (c - 1) % CF)

            for c in range(CF):
                step(c, c)
            with dve.Fori(1, E) as e:
                for c in range(CF):
                    step(e * CF + c, c)
            hidden_sum(NCH - 1, CF - 1)

            dve.wait_ge(b2_ready, 1)
            dve.wait_ge(down_done, NCH)
            for half in range(2):
                nc.vector.scalar_tensor_tensor(y[:, half], down_ps[:, half], b2_twice[:, 0:1], h1[:, half],
                                               ALU.add, ALU.add).then_inc(y_ready, 1)

        @block.gpsimd
        def _(pool):
            for m in range(6):
                pool.wait_ge(qkv_in[m], 16)
                nc.gpsimd.tensor_scalar(w_qkv_hi[:, m], w_qkv_sb[:, m], 1.0, 0.0, ALU.mult, ALU.add)\
                    .then_inc(qkv_hi_ready, 1)
                pool.wait_ge(qkv_hi_ready, m + 1)
                nc.gpsimd.tensor_tensor(w_qkv_lo[:, m], w_qkv_sb[:, m], w_qkv_hi[:, m].bitcast(F32), ALU.subtract)\
                    .then_inc(qkv_split, 1)

            def split_w1(e, slot):
                h = 2 * e + slot
                src = w1_sb[:, bass.ds(h * 2 * P, 2 * P)]
                if not (isinstance(h, int) and h < 2):
                    pool.wait_ge(up_done, 2 * h - 2)
                nc.gpsimd.tensor_copy(w1_hi[:, slot], src).then_inc(w1hi_ready, 1)
                pool.wait_ge(w1hi_ready, h + 1)
                pool.nop(nofuse=True)
                nc.gpsimd.tensor_tensor(w1_lo[:, slot], src, w1_hi[:, slot].bitcast(F32), ALU.subtract)\
                    .then_inc(w1_split, 1)

            def take_w2(e, slot):
                h = 2 * e + slot
                if not (isinstance(h, int) and h < 2):
                    pool.wait_ge(down_done, 2 * h - 2)
                pool.nop(nofuse=True)
                nc.gpsimd.tensor_copy(w2_ring[:, slot], w2_sb[:, bass.ds(h * 2 * P, 2 * P)]).then_inc(w2_ready, 1)

            pool.wait_ge(w1_in, 16)
            pool.wait_ge(w2_in, 16)
            pool.wait_ge(part_done, 2 * NQK + B // 2)
            for slot in range(2):
                split_w1(0, slot)
            for slot in range(2):
                take_w2(0, slot)
            for slot in range(2):
                split_w1(1, slot)
            with pool.Fori(1, E - 1) as e:
                for slot in range(2):
                    take_w2(e, slot)
                    split_w1(e + 1, slot)
            for slot in range(2):
                take_w2(E - 1, slot)

        @block.sync
        def _(sp):
            sp.dma_start(tok_w_sb[:], tok_w).then_inc(tokw_in, 16)
            for k in range(KP):
                sp.dma_start(patch_sb[:, k], patches[:, k]).then_inc(patch_in[k], 16)
                if k == 0:
                    sp.dma_start(small_sb[:], small).then_inc(small_in, 16)
                if k == 2:
                    sp.dma_start(const_sb[:], consts).then_inc(const_in, 16)
            for m in range(6):
                sp.dma_start(w_qkv_sb[:, m], w_qkv[m]).then_inc(qkv_in[m], 16)
            sp.dma_start(w_out_sb[:], w_out).then_inc(wout_in, 16)
            sp.dma_start(w1_sb[:].rearrange("p (e f) -> p e f", e=E), w1).then_inc(w1_in, 16)
            sp.dma_start(w2_sb[:], w2).then_inc(w2_in, 16)
            for half in range(2):
                sp.wait_ge(y_ready, half + 1)
                sp.dma_start(out[:, half * HT:(half + 1) * HT], y[:, half]).then_inc(stored, 16)
            sp.wait_ge(stored, 32)


def constants(S):
    import numpy as np

    row, col = np.arange(S)[:, None], np.arange(S)[None, :]
    scale = np.float32(64) ** -0.5
    masks = np.zeros((P, 3, S), np.float32)
    for base in (0, 64):
        masks[base:base + S, 0] = np.where(row <= col, scale, 0)
        masks[base:base + S, 1] = np.where(row > col, 0.5, 0)
        masks[base:base + S, 2] = np.where(col <= row, 0, NEG)
    center = np.eye(P) - 1.0 / P
    return np.concatenate([center, np.eye(P), masks.reshape(P, 3 * S)], axis=1).astype(np.float32)


def kernel(**inputs):
    import numpy as np
    import concourse.bacc as bacc
    from concourse.bass_utils import run_bass_kernel_spmd

    x = np.asarray(inputs["x"])
    B, C, H, W = x.shape
    pz = 16
    D = inputs["L0_tok_w"].shape[0]
    hp, wp = H // pz, W // pz
    S = hp * wp
    E, _, DFF = inputs["L0_ffn_W1"].shape
    K = C * pz * pz
    KP = K // P
    HD = inputs["L0_attn_w_q_u"].shape[1]
    dims = dict(B=B, S=S, D=D, HEADS=HD // 64, DH=64, E=E, DFF=DFF, KP=KP)

    def a(name):
        return np.asarray(inputs[name])

    patches = x.reshape(B, C, hp, pz, wp, pz).transpose(1, 3, 5, 0, 2, 4).reshape(KP, P, B * S).transpose(1, 0, 2)
    tok_w = a("L0_tok_w").T.reshape(KP, P, D).transpose(1, 0, 2)
    small = np.concatenate([a("L0_tok_b").reshape(P, 1), a("L0_ffn_b2").T, a("L0_ffn_Wg"),
                            a("L0_ffn_b1").reshape(E * DFF // P, P).T], axis=1)
    arrays = {
        "patches": patches, "tok_w": tok_w, "consts": constants(S), "small": small,
        "w_out": a("L0_attn_w_out").reshape(HD // P, P, D).transpose(1, 0, 2),
        "w1": a("L0_ffn_W1").transpose(1, 0, 2),
        "w2": a("L0_ffn_W2").reshape(E * DFF // P, P, D).transpose(1, 0, 2).reshape(P, E * DFF),
    }
    for n in ("q_u", "k_u", "v_u", "q_c", "k_c", "v_c"):
        arrays[f"w_{n}"] = a(f"L0_attn_w_{n}")
    arrays = {k: np.ascontiguousarray(v) for k, v in arrays.items()}
    nc = bacc.Bacc("TRN2", target_bir_lowering=False, num_devices=1)
    ap = {k: nc.dram_tensor(k, v.shape, mybir.dt.from_np(v.dtype), kind="ExternalInput").ap() for k, v in arrays.items()}
    out = nc.dram_tensor("out", (D, B * S), F32, kind="ExternalOutput").ap()
    vit_layer(nc, ap["patches"], ap["tok_w"], ap["consts"], ap["small"],
              [ap[f"w_{n}"] for n in ("q_u", "k_u", "v_u", "q_c", "k_c", "v_c")],
              ap["w_out"], ap["w1"], ap["w2"], out, dims)
    r = run_bass_kernel_spmd(nc, [arrays], core_ids=[0])
    return r.results[0]["out"].T.reshape(B, S, D)
```

```python
from contextlib import ExitStack

import concourse.bass as bass
from concourse import mybir

P = 128
F32 = mybir.dt.float32
F32R = mybir.dt.float32r
ALU = mybir.AluOpType
ACT = mybir.ActivationFunctionType
AX_X = mybir.AxisListType.X
EPS = 1e-5
NEG = -1e30

QU, KU, VU, QC, KC, VC = range(6)


def vit_layer(nc, patches, tok_w, consts, small, w_qkv, w_out, w1, w2, out, dims):
    B, S, D, HEADS, DH, E, DFF, KP = (dims[k] for k in ("B", "S", "D", "HEADS", "DH", "E", "DFF", "KP"))
    T = B * S
    HT = T // 2
    CH = HEADS * DH // P
    CF = DFF // P
    NB = 4
    NG = B // NB
    GT = NB * S
    ROWS = P
    BLK = CH * (NB // 2)
    WIDE = BLK * S
    TT = 96
    NT = T // TT
    NCH = E * CF
    SCALE = float(DH) ** -0.5
    assert D == P and DH == 64 and S <= 64 and WIDE <= 512 and HT <= 512 and NT * TT == T and CF == 4

    with ExitStack() as ctx:
        def sb(name, shape, dt=F32):
            return ctx.enter_context(nc.sbuf_tensor(name, shape, dt))

        def sem(name):
            return ctx.enter_context(nc.semaphore(name))

        ps = ctx.enter_context(nc.psum_tensor("ps", [P, 8, 512], F32))

        patch_sb = sb("patch_sb", [P, KP, T])
        tok_w_sb = sb("tok_w_sb", [P, KP, D])
        const_sb = sb("const_sb", [P, 2 * P + 3 * S])
        small_sb = sb("small_sb", [P, 1 + 2 * E + E * CF])
        centering = const_sb[:, 0:P]
        ident = const_sb[:, P:2 * P]
        tok_b = small_sb[:, 0:1]
        b2_sb = small_sb[:, 1:1 + E]
        w_gate = small_sb[:, 1 + E:1 + 2 * E]
        b1_sb = small_sb[:, 1 + 2 * E:1 + 2 * E + E * CF]
        w_qkv_sb = sb("w_qkv_sb", [P, 6, CH * P])
        w_qkv_hi = sb("w_qkv_hi", [P, 6, CH * P], F32R)
        w_qkv_lo = sb("w_qkv_lo", [P, 6, CH * P], F32R)
        w_out_sb = sb("w_out_sb", [P, CH, D])
        w1_sb = sb("w1_sb", [P, E * DFF])
        w2_sb = sb("w2_sb", [P, E * DFF])
        mean_w = sb("mean_w", [P, P])
        ones = sb("ones", [P, P])
        masks = sb("masks", [P, 3, BLK, S])
        gate_mask, look_mask, causal_mask = (masks[0:ROWS, k].rearrange("p n s -> p (n s)") for k in range(3))

        h0 = sb("h0", [P, 2, HT])
        h1 = sb("h1", [P, 2, HT])
        sq = sb("sq", [P, 2, HT])
        xc = sb("xc", [P, 2, HT])
        eps = sb("eps", [P, 1])
        sd = sb("sd", [P, NT])
        rstd = sb("rstd", [P, NT])
        xn = sb("xn", [P, T])

        x_hi = sb("x_hi", [P, B, 64], F32R)
        x_lo = sb("x_lo", [P, B, 64], F32R)
        qk = sb("qk", [P, 5, CH, T])
        v_sb = sb("v_sb", [P, B // 2, CH * P])
        gate = sb("gate", [P, 2, WIDE])
        look = sb("look", [P, 2, WIDE])
        sc_m = sb("sc_m", [P, 2, WIDE])
        soft = sb("soft", [P, 2, 2, WIDE])
        prob_t = sb("prob_t", [P, 2, BLK, 2, S])
        row_max = sb("row_max", [P, 2 * BLK])
        row_sum = sb("row_sum", [P, 2 * BLK])
        row_inv = sb("row_inv", [P, 2 * BLK])
        o_t = sb("o_t", [P, CH, T])

        g_max = sb("g_max", [P, NT])
        g_shift = sb("g_shift", [P, NT, E])
        g_exp = sb("g_exp", [P, NT, E])
        g_sum = sb("g_sum", [P, NT])
        g_inv = sb("g_inv", [P, NT])
        g_top = sb("g_top", [P, NT, 8])
        g_share = sb("g_share", [P, NT, 2])
        g_two = sb("g_two", [P, NT])
        g_twoi = sb("g_twoi", [P, NT])
        g_pn = sb("g_pn", [P, NT, 2])
        g_p0i = sb("g_p0i", [P, NT])
        g_ratio = sb("g_ratio", [P, NT])
        diag = sb("diag", [P, 2, NT, TT])
        late = qk[:].rearrange("p a b t -> p (a b) t")
        xn2 = late[:, 0]
        xs, ratio = (late[:, k].rearrange("p (h t) -> p h t", h=2) for k in (1, 2))

        def halves(tile, slots, start=0):
            flat = tile[:].rearrange("p a b -> p (a b)")[:, start:start + slots * T]
            return flat.rearrange("p (s h t) -> p s h t", s=slots, h=2)

        ga, gb = halves(patch_sb, 4), halves(patch_sb, 2, 4 * T)
        zb = halves(w_qkv_sb, 2)
        hid = late[:, 3:3 + CF].rearrange("p c (h t) -> p c h t", h=2)

        def split_parts(tile):
            w = tile[:].rearrange("p a b -> p (a b)")[:, T:T + 4 * P]
            return halves(tile, 1)[:, 0], w.rearrange("p (s n) -> p s n", s=2)

        xs_hi, w1_hi = split_parts(w_qkv_hi)
        xs_lo, w1_lo = split_parts(w_qkv_lo)
        w2_ring = sb("w2_ring", [P, 2, 2 * P])
        b2_sum = sb("b2_sum", [P, 1])
        b2_twice = sb("b2_twice", [P, 1])
        y = xs

        const_in, small_in = sem("const_in"), sem("small_in")
        tokw_in = [sem(f"tokw_in{k}") for k in range(KP // 2)]
        patch_in = [[sem(f"patch_in{half}_{k}") for k in range(KP // 2)] for half in range(2)]
        qkv_in = [sem(f"qkv_in{k}") for k in range(6)]
        wout_in, w1_in, w2_in = sem("wout_in"), sem("w1_in"), sem("w2_in")
        stored = sem("stored")
        psum_clear, fills, masks_ready, zeros_ready = sem("psum_clear"), sem("fills"), sem("masks_ready"), sem("zeros_ready")
        lo_clear, prob_clear = sem("lo_clear"), sem("prob_clear")
        qkv_hi_ready, qkv_split = sem("qkv_hi_ready"), sem("qkv_split")
        first_hi_ready, first_split = sem("first_hi_ready"), sem("first_split")
        emb_done, res_ready = sem("emb_done"), sem("res_ready")
        cen_done, xc_ready, sq_ready, var_done, sd_ready, rstd_ready, ndiag_ready, norm_mm, xn_ready = (
            sem("cen_done"), sem("xc_ready"), sem("sq_ready"), sem("var_done"), sem("sd_ready"), sem("rstd_ready"),
            sem("ndiag_ready"), sem("norm_mm"), sem("xn_ready"))
        xhi_ready, x_split = sem("xhi_ready"), sem("x_split")
        part_done = sem("part_done")
        part_taken = [sem(f"part_taken{b}") for b in range(4)]
        look_done, sc_done, gate_done, su_done = sem("look_done"), sem("sc_done"), sem("gate_done"), sem("su_done")
        lookt_ready, look_ready, scm_ready, gate_ready = (
            sem("lookt_ready"), sem("look_ready"), sem("scm_ready"), sem("gate_ready"))
        sut_ready, su_ready, logit_ready, max_ready, shift_ready, exp_ready, sum_ready, inv_ready, prob_ready = (
            sem("sut_ready"), sem("su_ready"), sem("logit_ready"), sem("max_ready"), sem("shift_ready"),
            sem("exp_ready"), sem("sum_ready"), sem("inv_ready"), sem("prob_ready"))
        pt_done, pt_ready, pv_done, o_ready = sem("pt_done"), sem("pt_ready"), sem("pv_done"), sem("o_ready")
        proj_done = sem("proj_done")
        route_mm, route_step, route_exp, diag_ready, share_mm = (
            sem("route_mm"), sem("route_step"), sem("route_exp"), sem("diag_ready"), sem("share_mm"))
        xs_ready, xshi_ready, xs_split, ratio_ready = sem("xs_ready"), sem("xshi_ready"), sem("xs_split"), sem("ratio_ready")
        w1hi_ready, w1_split, w2_ready = sem("w1hi_ready"), sem("w1_split"), sem("w2_ready")
        up_done, down_done, zb_ready, ga_ready, gb_ready, hid_ready = (
            sem("up_done"), sem("down_done"), sem("zb_ready"), sem("ga_ready"), sem("gb_ready"),
            sem("hid_ready"))
        lead_done, lead_ready = sem("lead_done"), sem("lead_ready")
        half_done = sem("half_done")
        b2s_ready, b2_ready, y_ready = sem("b2s_ready"), sem("b2_ready"), sem("y_ready")

        LEAD = 3
        ROUTE_STEPS = 10

        def pair(b, n):
            return ps[:, b:b + 2, 0:n]

        emb_ps = pair(0, HT)
        gate_ps, look_ps, sc_ps = pair(2, WIDE), pair(4, WIDE), pair(6, WIDE)
        su_ps, pt_ps, o_ps = gate_ps, look_ps, sc_ps
        attn_ps = pair(0, HT)
        HN = NT // 2

        def norm_banks(k, half):
            b, var = ((6 + half, 4 + half), (half, (0, 3)[half]))[k]
            return ps[:, b, 0:HT], ps[0:TT, var, 0:HN], ps[:, b, 0:HT]

        def route_ps(half):
            return ps[0:TT, half, 0:HN * E].rearrange("p (n e) -> p n e", n=HN)

        down_ps, up_ring = pair(0, HT), [pair(b, HT) for b in (2, 4, 6)]

        def up_ps(n, s):
            return up_ring[2 if isinstance(n, int) and n == 2 else s]

        NQK = 5 * CH
        LATER = ([("qk", k) for k in range(5)] + [("v", 0), ("qk", 5), ("qk", 6), ("v", 1)]
                 + [("qk", k) for k in range(7, NQK)] + [("v", pair) for pair in range(2, B // 2)])

        def part_qk(h, k):
            return k if h == 0 else NQK + LATER.index(("qk", k))

        def part_v(pair):
            return NQK + LATER.index(("v", pair))

        def bank(part):
            if part > part_v(4):
                return 1
            return part % 4 if part < NQK else part % 2

        EARLY_M = 2

        def by_vector(part):
            return part < NQK and part % 2 == 1

        def taken(eng, part):
            before = sum(bank(k) == bank(part) for k in range(part))
            eng.wait_ge(part_taken[bank(part)], before + 1)

        def bank_before(part):
            return max((k for k in range(part) if bank(k) == bank(part)), default=None)

        def split_mm(pe, dst, w, w_lo, x, x_lo, low_ready=None):
            pe.matmul(dst, w, x, start=True, stop=False)
            pe.matmul(dst, w_lo, x, start=False, stop=False)
            if low_ready:
                pe.wait_ge(*low_ready)
            return pe.matmul(dst, w, x_lo, start=False, stop=True)

        block = ctx.enter_context(nc.Block())

        @block.tensor
        def _(pe):
            def center(k, half):
                pe.wait_ge(res_ready, 2 * k + half + 1)
                pe.matmul(norm_banks(k, half)[0], centering, (h0, h1)[k][:, half], start=True, stop=True)\
                    .then_inc(cen_done, 1)

            def variance(k, half):
                pe.wait_ge(sq_ready, 2 * k + half + 1)
                if k == 1 and half == 0:
                    pe.wait_ge(xc_ready, 2 * k + half + 1)
                for n in range(HN):
                    mm = pe.matmul(norm_banks(k, half)[1][:, n:n + 1], sq[:, half, n * TT:(n + 1) * TT],
                                   mean_w[:, 0:1], start=True, stop=True)
                mm.then_inc(var_done, 1)

            def spread_deviation(k, half):
                pe.wait_ge(ndiag_ready, 2 * k + half + 1)
                spread(norm_banks(k, half)[2], 0, half).then_inc(norm_mm, 1)

            def spread(dst, k, half):
                tiles = slice(half * HN, (half + 1) * HN)
                return pe.matmul(dst, ones[0:TT, :], diag[0:TT, k, tiles].rearrange("p n t -> p (n t)"),
                                 start=True, stop=True)

            def embed(half, first, last):
                for k in range(2 * first, 2 * last):
                    if k % 2 == 0:
                        if half == 0:
                            pe.wait_ge(tokw_in[k // 2], 16)
                        pe.wait_ge(patch_in[half][k // 2], 16)
                    mm = pe.matmul(emb_ps[:, half], tok_w_sb[:, k], patch_sb[:, k, half * HT:(half + 1) * HT],
                                   start=(k == 0), stop=(k == KP - 1))
                if last == KP // 2:
                    mm.then_inc(emb_done, 1)

            def project_later(*numbers):
                for n in numbers:
                    kind, which = LATER[n]
                    if kind == "qk":
                        project_qk(1, which, which + 1)
                    else:
                        project_v(which)

            def project_qk(h, first, last):
                pe.wait_ge(xhi_ready, h + 1)
                for k in range(first, last):
                    m, c = divmod(k, CH)
                    part = part_qk(h, k)
                    if h == 0 and c == 0:
                        if m < EARLY_M:
                            pe.wait_ge(first_split, m + 1)
                        else:
                            pe.wait_ge(qkv_split, m - EARLY_M + 1)
                    if bank_before(part) is not None:
                        taken(pe, bank_before(part))
                    ch, two = slice(c * P, (c + 1) * P), slice(h * B // 2, (h + 1) * B // 2)
                    split_mm(pe, ps[:, bank(part), 0:HT], w_qkv_hi[:, m, ch], w_qkv_lo[:, m, ch],
                             x_hi[:, two, 0:S], x_lo[:, two, 0:S],
                             low_ready=(x_split, h + 1) if k == 0 else None).then_inc(part_done, 1)

            def project_v(pair):
                part = part_v(pair)
                pe.wait_ge(qkv_split, 6 - EARLY_M)
                taken(pe, bank_before(part))
                two = slice(2 * pair, 2 * pair + 2)
                split_mm(pe, ps[:, bank(part), :], x_hi[:, two].rearrange("p b s -> p (b s)"),
                         x_lo[:, two].rearrange("p b s -> p (b s)"),
                         w_qkv_hi[:, VC], w_qkv_lo[:, VC]).then_inc(part_done, 1)

            def by_head(g, dst, a, b):
                for blk in range(BLK):
                    c, q = divmod(blk, NB // 2)
                    for hp in range(2):
                        for bp in range(2):
                            at = g * GT + (2 * q + bp) * S
                            rows = slice(64 * hp, 64 * hp + 64)
                            mm = pe.matmul(dst[64 * bp:64 * bp + S, hp, blk * S:(blk + 1) * S],
                                           qk[rows, a, c, at:at + S], qk[rows, b, c, at:at + S], start=True, stop=True)
                return mm

            def projected(g, *projections):
                for m in projections:
                    for c in range(CH):
                        taken(pe, part_qk(g // 2, m * CH + c))

            def look_scores(g):
                projected(g, QU, KU)
                if g == 1:
                    pe.wait_ge(lookt_ready, 1)
                if g >= 2:
                    pe.wait_ge(pt_ready, 2 * (g - 1))
                by_head(g, look_ps, KU, QU).then_inc(look_done, 1)

            def gate_scores(g):
                projected(g, VU, QC)
                if g == 0:
                    projected(g, KC)
                else:
                    pe.wait_ge(su_ready, g)
                by_head(g, gate_ps, VU, QC).then_inc(gate_done, 1)

            def causal_scores(g):
                projected(g, QC, KC)
                if g == 1:
                    pe.wait_ge(scm_ready, 1)
                if g >= 2:
                    pe.wait_ge(o_ready, 2 * (g - 1))
                by_head(g, sc_ps, QC, KC).then_inc(sc_done, 1)

            def gate_sums(g):
                pe.wait_ge(look_ready, g + 1)
                pe.wait_ge(gate_ready, g + 1)
                for hp in range(2):
                    for blk in range(BLK):
                        for bp in range(2):
                            rows, cols = slice(64 * bp, 64 * bp + 64), slice(blk * S, (blk + 1) * S)
                            mm = pe.matmul(su_ps[64 * bp:64 * bp + S, hp, cols], gate[rows, hp, cols],
                                           look[rows, hp, cols], start=True, stop=True)
                mm.then_inc(su_done, 1)

            def transpose_probs(g):
                if g < NG - 1:
                    pe.wait_ge(lookt_ready, g + 2)
                else:
                    pe.wait_ge(pt_ready, 2 * g)
                for hp in range(2):
                    pe.wait_ge(prob_ready, 2 * g + hp + 1)
                    for blk in range(BLK):
                        for bp in range(2):
                            rows, cols = slice(64 * bp, 64 * bp + 64), slice(blk * S, (blk + 1) * S)
                            mm = pe.matmul(pt_ps[64 * bp:64 * bp + S, hp, cols], soft[rows, g % 2, hp, cols],
                                           ident[rows, 64 * bp:64 * bp + S], start=True, stop=True)
                    mm.then_inc(pt_done, 1)

            def weighted_values(g):
                if g < NG - 1:
                    pe.wait_ge(scm_ready, g + 2)
                else:
                    pe.wait_ge(o_ready, 2 * g)
                for q in range(2):
                    taken(pe, part_v(2 * g + q))
                for hp in range(2):
                    pe.wait_ge(pt_ready, 2 * g + hp + 1)
                    for blk in range(BLK):
                        c, q = divmod(blk, NB // 2)
                        head = slice((2 * c + hp) * 64, (2 * c + hp + 1) * 64)
                        mm = pe.matmul(o_ps[64 * hp:64 * hp + 64, q, c * 2 * S:(c + 1) * 2 * S],
                                       v_sb[:, 2 * g + q, head], prob_t[:, hp, blk], start=True, stop=True)
                mm.then_inc(pv_done, 1)

            def project_out(g):
                half = g // 2
                cols = slice(g % 2 * GT, (g % 2 + 1) * GT)
                pe.wait_ge(o_ready, 2 * (g + 1))
                pe.wait_ge(wout_in, 16)
                taken(pe, part_v(B // 4) if half == 0 else part_v(B // 2 - 1))
                for c in range(CH):
                    mm = pe.matmul(attn_ps[:, half, cols], w_out_sb[:, c], o_t[:, c, g * GT:(g + 1) * GT],
                                   start=(c == 0), stop=(c == CH - 1))
                mm.then_inc(proj_done, 1)

            def route(half):
                pe.wait_ge(xn_ready, 3 + half)
                for n in range(HN):
                    at = half * HT + n * TT
                    mm = pe.matmul(route_ps(half)[:, n], xn2[:, at:at + TT], w_gate, start=True, stop=True)
                mm.then_inc(route_mm, 1)

            def spread_share(half):
                pe.wait_ge(diag_ready, 2 * half + 1)
                spread(ps[:, half, 0:HT], 0, half).then_inc(share_mm, 1)

            def spread_ratio(half):
                pe.wait_ge(diag_ready, 2 * half + 2)
                pe.wait_ge(xs_ready, half + 1)
                spread(ps[:, half, 0:HT], 1, half).then_inc(share_mm, 1)

            def up(e, c, halves=(0, 1)):
                n = e * CF + c
                slot, at = c // 2, slice((c % 2) * P, (c % 2 + 1) * P)
                pe.wait_ge(w1_split, 2 * e + slot + 1)
                if isinstance(n, int) and n == CF:
                    pe.wait_ge(zb_ready, 1)
                elif not (isinstance(n, int) and n < 3):
                    pe.wait_ge(zb_ready, n - 1)
                for half in halves:
                    first = isinstance(n, int) and n == 0
                    if first:
                        pe.wait_ge(xshi_ready, half + 1)
                    mm = split_mm(pe, up_ps(n, c % 2)[:, half], w1_hi[:, slot, at], w1_lo[:, slot, at],
                                  xs_hi[:, half], xs_lo[:, half], low_ready=(xs_split, half + 1) if first else None)
                mm.then_inc(up_done if 1 in halves else lead_done, 1)

            def keep_warm(bank, n):
                for _ in range(n):
                    pe.matmul(ps[:, bank, :], x_hi[:, 0:2].rearrange("p b s -> p (b s)"),
                              x_hi[:, 0:8].rearrange("p b s -> p (b s)"), start=True, stop=True)

            pe.wait_ge(zeros_ready, 1)
            keep_warm(0, 8)

            embed(0, 0, 3)
            embed(1, 0, 1)
            pe.wait_ge(psum_clear, 2)
            pe.wait_ge(const_in, 16)
            center(0, 0)
            embed(1, 1, 2)
            pe.wait_ge(fills, 2)
            variance(0, 0)
            embed(1, 2, 3)
            spread_deviation(0, 0)
            center(0, 1)
            project_qk(0, 0, 2)
            variance(0, 1)
            project_qk(0, 2, 4)
            spread_deviation(0, 1)
            project_qk(0, 4, NQK)

            look_scores(0)
            project_later(0, 1)
            gate_scores(0)
            project_later(2)
            causal_scores(0)
            project_later(3, 4)
            gate_sums(0)
            project_later(5)
            look_scores(1)
            project_later(6, 7)
            gate_scores(1)
            project_later(8)
            causal_scores(1)
            project_later(9, 10)
            gate_sums(1)
            project_later(11, 12, 13)
            transpose_probs(0)
            project_later(14, 15)
            weighted_values(0)
            project_later(16, 17, 18)
            look_scores(2)
            project_later(19, 20, 21)
            gate_scores(2)
            project_later(22)
            causal_scores(2)
            gate_sums(2)
            project_later(23)
            transpose_probs(1)
            weighted_values(1)
            project_later(24)
            look_scores(3)
            project_out(0)
            project_later(25)
            project_out(1)
            gate_scores(3)
            center(1, 0)
            taken(pe, part_v(5))
            keep_warm(1, 1)
            project_later(26)
            causal_scores(3)
            variance(1, 0)
            gate_sums(3)
            taken(pe, part_v(6))
            keep_warm(1, 1)
            project_later(27)
            transpose_probs(2)
            spread_deviation(1, 0)
            weighted_values(2)
            route(0)
            project_out(2)
            pe.wait_ge(su_ready, 4)
            keep_warm(2, 2)
            transpose_probs(3)
            weighted_values(3)
            spread_share(0)
            project_out(3)
            keep_warm(5, 2)
            center(1, 1)
            spread_ratio(0)
            variance(1, 1)
            for c in range(LEAD - 1):
                up(0, c, halves=(0,))
            keep_warm(5, 1)
            spread_deviation(1, 1)
            up(0, LEAD - 1, halves=(0,))
            keep_warm(5, 1)
            route(1)
            keep_warm(5, 14)
            spread_share(1)
            keep_warm(5, 3)
            spread_ratio(1)

            def down(e, c):
                n = e * CF + c
                slot, at = c // 2, slice((c % 2) * P, (c % 2 + 1) * P)
                first, last = isinstance(n, int) and n == 0, isinstance(n, int) and n == NCH - 1
                pe.wait_ge(w2_ready, 2 * e + slot + 1)
                pe.wait_ge(hid_ready, n + 1)
                for half in range(2):
                    mm = pe.matmul(down_ps[:, half], w2_ring[:, slot, at], hid[:, c, half], start=first, stop=last)
                    if last and half == 0:
                        mm.then_inc(half_done, 1)
                mm.then_inc(down_done, 1)

            for c in range(CF):
                up(0, c, halves=(1,) if c < LEAD else (0, 1))
            pe.wait_ge(ratio_ready, 2)
            for c in range(CF):
                up(1, c)
                down(0, c)
            with pe.Fori(1, E - 1) as e:
                for c in range(CF):
                    up(e + 1, c)
                    down(e, c)
            for c in range(CF):
                down(E - 1, c)

        @block.scalar
        def _(act):
            nc.scalar.preload_act_table(ACT.Sqrt)
            act.wait_ge(small_in, 16)
            def take_embedded(half):
                act.wait_ge(emb_done, half + 1)
                nc.scalar.activation(h0[:, half], emb_ps[:, half], ACT.Identity, bias=tok_b).then_inc(res_ready, 1)

            def square(k, half):
                act.wait_ge(cen_done, 2 * k + half + 1)
                nc.scalar.activation(sq[:, half], norm_banks(k, half)[0], ACT.Square).then_inc(sq_ready, 1)

            def deviation(k, half):
                act.wait_ge(var_done, 2 * k + half + 1)
                nc.scalar.activation(sd[0:TT, half * HN:(half + 1) * HN], norm_banks(k, half)[1], ACT.Sqrt,
                                     bias=eps[0:TT]).then_inc(sd_ready, 1)

            def take_qk(h, first, last):
                for k in range(first, last):
                    m, c = divmod(k, CH)
                    part = part_qk(h, k)
                    if by_vector(part):
                        continue
                    act.wait_ge(part_done, part + 1)
                    nc.scalar.copy(qk[:, m, c, h * HT:(h + 1) * HT], ps[:, bank(part), 0:HT])\
                        .then_inc(part_taken[bank(part)], 1)

            def take_v(pair):
                act.wait_ge(part_done, part_v(pair) + 1)
                nc.scalar.copy(v_sb[:, pair], ps[:, bank(part_v(pair)), :]).then_inc(part_taken[bank(part_v(pair))], 1)

            def take_later(*numbers):
                for n in numbers:
                    kind, which = LATER[n]
                    if kind == "qk":
                        take_qk(1, which, which + 1)
                    else:
                        take_v(which)

            def lookahead(g):
                act.wait_ge(look_done, g + 1)
                if g >= 1:
                    act.wait_ge(su_done, g)
                nc.scalar.activation(look[0:ROWS], look_ps[0:ROWS], ACT.Tanh, scale=SCALE / 2)\
                    .then_inc(lookt_ready, 1)

            def gate_tanh(g):
                act.wait_ge(su_done, g + 1)
                if g >= 2:
                    act.wait_ge(pt_done, 2 * (g - 1))
                nc.scalar.activation(soft[0:ROWS, g % 2], su_ps[0:ROWS], ACT.Tanh, scale=0.5).then_inc(sut_ready, 1)

            def exponent(g):
                act.wait_ge(shift_ready, g + 1)
                nc.scalar.activation(soft[0:ROWS, g % 2], soft[0:ROWS, g % 2], ACT.Exp, scale=SCALE).then_inc(exp_ready, 1)

            def take_probs(g):
                for hp in range(2):
                    act.wait_ge(pt_done, 2 * g + hp + 1)
                    if g == 0:
                        act.wait_ge(prob_clear, 1)
                    if g >= 1:
                        act.wait_ge(pv_done, g)
                    for bp in range(2):
                        rows = slice(64 * bp, 64 * bp + S)
                        ins = nc.scalar.copy(prob_t[rows, hp, :, bp], pt_ps[rows, hp].rearrange("p (n s) -> p n s", s=S))
                    ins.then_inc(pt_ready, 1)

            def take_o(g):
                act.wait_ge(pv_done, g + 1)
                for q in range(2):
                    at = o_t[:].rearrange("p c (g q w) -> p c g q w", g=NG, q=2)
                    nc.scalar.copy(at[:, :, g, q], o_ps[:, q].rearrange("p (c w) -> p c w", c=CH)).then_inc(o_ready, 1)

            def route_exponent(half):
                act.wait_ge(route_step, half * ROUTE_STEPS + 2)
                tiles = slice(half * HN, (half + 1) * HN)
                nc.scalar.activation(g_exp[0:TT, tiles], g_shift[0:TT, tiles], ACT.Exp).then_inc(route_exp, 1)

            def take_ratio(half):
                act.wait_ge(share_mm, 2 * half + 2)
                nc.scalar.copy(ratio[:, half], ps[:, half, 0:HT]).then_inc(ratio_ready, 1)

            take_embedded(0)
            square(0, 0)
            act.wait_ge(fills, 3)
            deviation(0, 0)
            take_embedded(1)
            square(0, 1)
            take_qk(0, 0, 2)
            deviation(0, 1)
            nc.scalar.preload_act_table(ACT.Tanh)
            take_qk(0, 2, NQK)
            lookahead(0)
            take_later(0, 1, 2, 3, 4)
            gate_tanh(0)
            take_later(5)
            lookahead(1)
            take_later(6, 7)
            exponent(0)
            take_later(8, 9, 10)
            gate_tanh(1)
            take_later(11, 12, 13)
            take_probs(0)
            take_later(14, 15)
            exponent(1)
            take_o(0)
            take_later(16, 17, 18)
            lookahead(2)
            take_later(19, 20, 21, 22)
            gate_tanh(2)
            take_later(23)
            take_probs(1)
            take_o(1)
            take_later(24)
            exponent(2)
            lookahead(3)
            take_later(25)
            square(1, 0)
            nc.scalar.preload_act_table(ACT.Sqrt)
            take_later(26)
            deviation(1, 0)
            nc.scalar.preload_act_table(ACT.Tanh)
            gate_tanh(3)
            take_later(27)
            take_probs(2)
            exponent(3)
            take_o(2)
            route_exponent(0)
            nc.scalar.preload_act_table(ACT.Sqrt)
            take_probs(3)
            take_o(3)
            square(1, 1)
            take_ratio(0)
            deviation(1, 1)
            nc.scalar.preload_act_table(ACT.Exp)
            route_exponent(1)
            nc.scalar.preload_act_table(ACT.Gelu)
            for n in range(LEAD):
                act.wait_ge(lead_done, n + 1)
                nc.scalar.activation(ga[:, n, 0], up_ps(n, n % 2)[:, 0], ACT.Gelu, bias=b1_sb[:, n:n + 1])\
                    .then_inc(lead_ready, 1)
            take_ratio(1)

            def gelu_first(n, c):
                s = c % 2
                act.wait_ge(up_done, n + 1)
                if not (isinstance(n, int) and n < 4):
                    act.wait_ge(hid_ready, n - 3)
                act.nop(nofuse=True)
                halves = slice(1, 2) if isinstance(n, int) and n < LEAD else slice(0, 2)
                nc.scalar.activation(ga[:, c, halves], up_ps(n, s)[:, halves], ACT.Gelu, bias=b1_sb[:, bass.ds(n, 1)]).then_inc(ga_ready, 1)

            def gelu_second(n, s):
                act.wait_ge(zb_ready, n + 1)
                if not (isinstance(n, int) and n < 2):
                    act.wait_ge(hid_ready, n - 1)
                act.nop(nofuse=True)
                nc.scalar.activation(gb[:, s], zb[:, s], ACT.Gelu, bias=b1_sb[:, bass.ds(n, 1)]).then_inc(gb_ready, 1)

            def step(n, c):
                s = c % 2
                gelu_first(n, c)
                if not (isinstance(n, int) and n < 1):
                    gelu_second(n - 1, 1 - s)

            for c in range(CF):
                step(c, c)
            with act.Fori(1, E) as e:
                for c in range(CF):
                    step(e * CF + c, c)
            gelu_second(NCH - 1, 1)

        @block.vector
        def _(dve):
            nc.vector.memset(x_hi[:].bitcast(F32), 0.0).then_inc(zeros_ready, 1)
            nc.vector.memset(mean_w[:], 1.0 / D).then_inc(fills, 1)
            nc.vector.memset(ones[:], 1.0).then_inc(fills, 1)
            nc.vector.memset(eps[:], EPS).then_inc(fills, 1)
            for above in (32, 96):
                nc.vector.memset(ps[above:above + 32, 2:8, 0:WIDE], 0.0).then_inc(psum_clear, 1)
            dve.wait_ge(const_in, 16)
            nc.vector.tensor_copy(
                masks[:], const_sb[:, 2 * P:].rearrange("p (k o s) -> p k o s", k=3, o=1).broadcast_to([P, 3, BLK, S]))\
                .then_inc(masks_ready, 1)
            dve.wait_ge(small_in, 16)
            nc.vector.reduce_sum(b2_sum[:], b2_sb, AX_X).then_inc(b2s_ready, 1)
            dve.wait_ge(b2s_ready, 1)
            nc.vector.tensor_scalar(b2_twice[:], b2_sum[:], 2.0, None, ALU.mult).then_inc(b2_ready, 1)

            def take_centered(k, half):
                dve.wait_ge(sq_ready, 2 * k + half + 1)
                nc.vector.tensor_copy(xc[:, half], norm_banks(k, half)[0]).then_inc(xc_ready, 1)

            def deviation(k, half):
                tiles = slice(half * HN, (half + 1) * HN)
                dve.wait_ge(sd_ready, 2 * k + half + 1)
                nc.vector.reciprocal(rstd[0:TT, tiles], sd[0:TT, tiles]).then_inc(rstd_ready, 1)
                dve.wait_ge(rstd_ready, 2 * k + half + 1)
                spread_out(0, rstd, half).then_inc(ndiag_ready, 1)

            def normed(k, half):
                dve.wait_ge(xc_ready, 2 * k + half + 1)
                dve.wait_ge(norm_mm, 2 * k + half + 1)
                nc.vector.tensor_tensor((xn, xn2)[k][:, half * HT:(half + 1) * HT], xc[:, half],
                                        norm_banks(k, half)[2], ALU.mult).then_inc(xn_ready, 1)

            def spread_out(k, by_token, half):
                tiles, n = slice(half * HN, (half + 1) * HN), HN
                return nc.vector.tensor_tensor(
                    diag[0:TT, k, tiles],
                    ident[0:TT, 0:TT].rearrange("p (o t) -> p o t", o=1).broadcast_to([TT, n, TT]),
                    by_token[0:TT, tiles].rearrange("p (n o) -> p n o", o=1).broadcast_to([TT, n, TT]), ALU.mult)

            def split_x(h):
                images = slice(h * B // 2, (h + 1) * B // 2)
                x = xn[:, h * HT:(h + 1) * HT].rearrange("p (b s) -> p b s", s=S)
                dve.wait_ge(xn_ready, h + 1)
                nc.vector.tensor_copy(x_hi[:, images, 0:S], x).then_inc(xhi_ready, 1)
                dve.wait_ge(xhi_ready, h + 1)
                if h == 0:
                    dve.wait_ge(lo_clear, 1)
                nc.vector.tensor_tensor(x_lo[:, images, 0:S], x, x_hi[:, images, 0:S].bitcast(F32), ALU.subtract)\
                    .then_inc(x_split, 1)

            def take_qk(first, last):
                for part in filter(by_vector, range(first, last)):
                    m, c = divmod(part, CH)
                    dve.wait_ge(part_done, part + 1)
                    nc.vector.tensor_copy(qk[:, m, c, 0:HT], ps[:, bank(part), 0:HT])\
                        .then_inc(part_taken[bank(part)], 1)

            def over(mask):
                return mask.rearrange("p (o w) -> p o w", o=1).broadcast_to([ROWS, 2, WIDE])

            def wide(rows):
                return rows[0:ROWS].rearrange("p (n o) -> p n o", o=1).broadcast_to([ROWS, 2 * BLK, S])

            def soft_blocks(g):
                return soft[0:ROWS, g % 2].rearrange("p h (n s) -> p (h n) s", s=S)

            def mask_look(g):
                dve.wait_ge(lookt_ready, g + 1)
                nc.vector.scalar_tensor_tensor(look[0:ROWS], look[0:ROWS], 1.0, over(look_mask), ALU.add, ALU.mult)\
                    .then_inc(look_ready, 1)

            def mask_scores(g):
                dve.wait_ge(sc_done, g + 1)
                if g >= 1:
                    dve.wait_ge(logit_ready, g)
                nc.vector.tensor_tensor(sc_m[0:ROWS], sc_ps[0:ROWS], over(causal_mask), ALU.add)\
                    .then_inc(scm_ready, 1)

            def mask_gate(g):
                dve.wait_ge(gate_done, g + 1)
                if g >= 1:
                    dve.wait_ge(su_done, g)
                nc.vector.tensor_tensor(gate[0:ROWS], gate_ps[0:ROWS], over(gate_mask), ALU.mult)\
                    .then_inc(gate_ready, 1)

            def logits(g):
                dve.wait_ge(sut_ready, g + 1)
                nc.vector.scalar_tensor_tensor(soft[0:ROWS, g % 2], soft[0:ROWS, g % 2], 1.0, su_ps[0:ROWS], ALU.add, ALU.mult)\
                    .then_inc(su_ready, 1)
                dve.wait_ge(su_ready, g + 1)
                dve.wait_ge(scm_ready, g + 1)
                nc.vector.scalar_tensor_tensor(soft[0:ROWS, g % 2], soft[0:ROWS, g % 2], -0.5 / SCALE, sc_m[0:ROWS],
                                               ALU.mult, ALU.add).then_inc(logit_ready, 1)
                dve.wait_ge(logit_ready, g + 1)
                nc.vector.tensor_reduce(row_max[0:ROWS], soft_blocks(g), AX_X, ALU.max).then_inc(max_ready, 1)
                dve.wait_ge(max_ready, g + 1)
                nc.vector.tensor_tensor(soft_blocks(g), soft_blocks(g), wide(row_max), ALU.subtract)\
                    .then_inc(shift_ready, 1)

            def row_sums(g):
                dve.wait_ge(exp_ready, g + 1)
                nc.vector.tensor_reduce(row_sum[0:ROWS], soft_blocks(g), AX_X, ALU.add).then_inc(sum_ready, 1)

            def normalise(g):
                dve.wait_ge(sum_ready, g + 1)
                nc.vector.reciprocal(row_inv[0:ROWS], row_sum[0:ROWS]).then_inc(inv_ready, 1)
                dve.wait_ge(inv_ready, g + 1)
                for hp in range(2):
                    soft_half = soft[0:ROWS, g % 2, hp].rearrange("p (n s) -> p n s", s=S)
                    inv = row_inv[0:ROWS, hp * BLK:(hp + 1) * BLK].rearrange("p (n o) -> p n o", o=1)
                    nc.vector.tensor_tensor(soft_half, soft_half, inv.broadcast_to([ROWS, BLK, S]), ALU.mult)\
                        .then_inc(prob_ready, 1)

            for m in range(EARLY_M):
                dve.wait_ge(qkv_in[m], 16)
                nc.vector.tensor_copy(w_qkv_hi[:, m], w_qkv_sb[:, m]).then_inc(first_hi_ready, 1)
                dve.wait_ge(first_hi_ready, m + 1)
                nc.vector.tensor_tensor(w_qkv_lo[:, m], w_qkv_sb[:, m], w_qkv_hi[:, m].bitcast(F32), ALU.subtract)\
                    .then_inc(first_split, 1)
            take_centered(0, 0)
            deviation(0, 0)
            normed(0, 0)
            split_x(0)
            take_centered(0, 1)
            take_qk(0, 2)
            deviation(0, 1)
            take_qk(2, 4)
            normed(0, 1)
            split_x(1)
            take_qk(4, NQK)
            dve.wait_ge(masks_ready, 1)
            mask_look(0)
            mask_gate(0)
            mask_scores(0)
            def residual(half):
                dve.wait_ge(proj_done, 2 * half + 2)
                nc.vector.tensor_tensor(h1[:, half], attn_ps[:, half], h0[:, half], ALU.add).then_inc(res_ready, 1)

            steps = 0

            def done(ins):
                nonlocal steps
                steps += 1
                ins.then_inc(route_step, 1)
                dve.wait_ge(route_step, steps)

            def over_experts(v):
                return v.rearrange("p (n o) -> p n o", o=1).broadcast_to([TT, HN, E])

            def of_half(tile, half):
                return tile[0:TT, half * HN:(half + 1) * HN]

            def router_logits(half):
                dve.wait_ge(route_mm, half + 1)
                done(nc.vector.tensor_reduce(of_half(g_max, half), route_ps(half), AX_X, ALU.max))
                done(nc.vector.tensor_tensor(of_half(g_shift, half), route_ps(half), over_experts(of_half(g_max, half)),
                                             ALU.subtract))

            def router_shares(half):
                t_exp, t_sum, t_inv, t_top, t_share, t_two, t_twoi, t_pn, t_p0i, t_ratio = (
                    of_half(t, half) for t in (g_exp, g_sum, g_inv, g_top, g_share, g_two, g_twoi, g_pn, g_p0i, g_ratio))

                def over_two(v):
                    return v.rearrange("p (n o) -> p n o", o=1).broadcast_to([TT, HN, 2])

                dve.wait_ge(route_exp, half + 1)
                for n in range(HN):
                    nc.vector.max(t_top[:, n], t_exp[:, n])
                done(nc.vector.tensor_reduce(t_sum, t_exp, AX_X, ALU.add))
                done(nc.vector.reciprocal(t_inv, t_sum))
                done(nc.vector.tensor_tensor(t_share, t_top[:, :, 0:2], over_two(t_inv), ALU.mult))
                done(nc.vector.tensor_tensor(t_two, t_share[:, :, 0], t_share[:, :, 1], ALU.add))
                done(nc.vector.reciprocal(t_twoi, t_two))
                done(nc.vector.tensor_tensor(t_pn, t_share, over_two(t_twoi), ALU.mult))
                spread_out(0, g_pn[:, :, 0], half).then_inc(diag_ready, 1)
                done(nc.vector.reciprocal(t_p0i, t_pn[:, :, 0]))
                done(nc.vector.tensor_tensor(t_ratio, t_pn[:, :, 1], t_p0i, ALU.mult))
                spread_out(1, g_ratio, half).then_inc(diag_ready, 1)
                assert steps == (half + 1) * ROUTE_STEPS

            def first_share(half):
                dve.wait_ge(share_mm, 2 * half + 1)
                nc.vector.tensor_tensor(xs[:, half], xn2[:, half * HT:(half + 1) * HT], ps[:, half, 0:HT], ALU.mult)\
                    .then_inc(xs_ready, 1)
                dve.wait_ge(xs_ready, half + 1)
                nc.vector.tensor_copy(xs_hi[:, half], xs[:, half]).then_inc(xshi_ready, 1)
                dve.wait_ge(xshi_ready, half + 1)
                nc.vector.tensor_tensor(xs_lo[:, half], xs[:, half], xs_hi[:, half].bitcast(F32), ALU.subtract)\
                    .then_inc(xs_split, 1)

            for g in range(2):
                logits(g)
                mask_look(g + 1)
                mask_gate(g + 1)
                row_sums(g)
                normalise(g)
                mask_scores(g + 1)
            logits(2)
            mask_look(3)
            residual(0)
            mask_gate(3)
            take_centered(1, 0)
            row_sums(2)
            normalise(2)
            deviation(1, 0)
            mask_scores(3)
            logits(3)
            normed(1, 0)
            row_sums(3)
            router_logits(0)
            normalise(3)
            router_shares(0)
            first_share(0)
            residual(1)
            take_centered(1, 1)
            deviation(1, 1)
            normed(1, 1)
            router_logits(1)
            router_shares(1)
            first_share(1)

            def lead_share(n, s):
                dve.wait_ge(ratio_ready, 1)
                dve.wait_ge(lead_ready, n + 1)
                nc.vector.tensor_tensor(zb[:, s, 0], up_ps(n, s)[:, 0], ratio[:, 0], ALU.mult)

            def second_share(n, s):
                if not (isinstance(n, int) and n < 2):
                    dve.wait_ge(gb_ready, n - 1)
                if isinstance(n, int) and n < LEAD:
                    if n >= 2:
                        lead_share(n, s)
                    dve.wait_ge(ratio_ready, 2)
                    dve.wait_ge(ga_ready, n + 1)
                    nc.vector.tensor_tensor(zb[:, s, 1], up_ps(n, s)[:, 1], ratio[:, 1], ALU.mult).then_inc(zb_ready, 1)
                else:
                    dve.wait_ge(ga_ready, n + 1)
                    nc.vector.tensor_tensor(zb[:, s], up_ps(n, s), ratio, ALU.mult).then_inc(zb_ready, 1)

            def hidden_sum(n, c):
                s = c % 2
                dve.wait_ge(gb_ready, n + 1)
                if not (isinstance(n, int) and n < CF):
                    dve.wait_ge(down_done, n - CF + 1)
                nc.vector.tensor_tensor(hid[:, c], ga[:, c], gb[:, s], ALU.add).then_inc(hid_ready, 1)

            def step(n, c):
                s = c % 2
                second_share(n, s)
                if not (isinstance(n, int) and n < 1):
                    hidden_sum(n - 1, (c - 1) % CF)

            for n in range(2):
                lead_share(n, n)
            for c in range(CF):
                step(c, c)
            with dve.Fori(1, E) as e:
                for c in range(CF):
                    step(e * CF + c, c)
            hidden_sum(NCH - 1, CF - 1)

            dve.wait_ge(b2_ready, 1)
            for half in range(2):
                if half == 0:
                    dve.wait_ge(half_done, 1)
                else:
                    dve.wait_ge(down_done, NCH)
                nc.vector.scalar_tensor_tensor(y[:, half], down_ps[:, half], b2_twice[:, 0:1], h1[:, half],
                                               ALU.add, ALU.add).then_inc(y_ready, 1)

        @block.gpsimd
        def _(pool):
            nc.gpsimd.memset(x_lo[:].bitcast(F32), 0.0).then_inc(lo_clear, 1)
            nc.gpsimd.memset(prob_t[:], 0.0).then_inc(prob_clear, 1)
            for m in range(EARLY_M, 6):
                pool.wait_ge(qkv_in[m], 16)
                nc.gpsimd.tensor_scalar(w_qkv_hi[:, m], w_qkv_sb[:, m], 1.0, 0.0, ALU.mult, ALU.add)\
                    .then_inc(qkv_hi_ready, 1)
                pool.wait_ge(qkv_hi_ready, m - EARLY_M + 1)
                nc.gpsimd.tensor_tensor(w_qkv_lo[:, m], w_qkv_sb[:, m], w_qkv_hi[:, m].bitcast(F32), ALU.subtract)\
                    .then_inc(qkv_split, 1)

            def split_w1(e, slot):
                h = 2 * e + slot
                src = w1_sb[:, bass.ds(h * 2 * P, 2 * P)]
                if not (isinstance(h, int) and h < 2):
                    pool.wait_ge(up_done, 2 * h - 2)
                nc.gpsimd.tensor_copy(w1_hi[:, slot], src).then_inc(w1hi_ready, 1)
                pool.wait_ge(w1hi_ready, h + 1)
                pool.nop(nofuse=True)
                nc.gpsimd.tensor_tensor(w1_lo[:, slot], src, w1_hi[:, slot].bitcast(F32), ALU.subtract)\
                    .then_inc(w1_split, 1)

            def take_w2(e, slot):
                h = 2 * e + slot
                if not (isinstance(h, int) and h < 2):
                    pool.wait_ge(down_done, 2 * h - 2)
                pool.nop(nofuse=True)
                nc.gpsimd.tensor_copy(w2_ring[:, slot], w2_sb[:, bass.ds(h * 2 * P, 2 * P)]).then_inc(w2_ready, 1)

            pool.wait_ge(w1_in, 16)
            pool.wait_ge(w2_in, 16)
            pool.wait_ge(part_done, 2 * NQK + B // 2)
            for slot in range(2):
                split_w1(0, slot)
            for slot in range(2):
                take_w2(0, slot)
            for slot in range(2):
                split_w1(1, slot)
            with pool.Fori(1, E - 1) as e:
                for slot in range(2):
                    take_w2(e, slot)
                    split_w1(e + 1, slot)
            for slot in range(2):
                take_w2(E - 1, slot)

        @block.sync
        def _(sp):
            def load_patches(half, k):
                cols = slice(half * HT, (half + 1) * HT)
                sp.dma_start(patch_sb[:, 2 * k:2 * k + 2, cols], patches[:, 2 * k:2 * k + 2, cols])\
                    .then_inc(patch_in[half][k], 16)

            def load_qkv(m):
                sp.dma_start(w_qkv_sb[:, m], w_qkv[m]).then_inc(qkv_in[m], 16)

            for k in range(KP // 2):
                sp.dma_start(tok_w_sb[:, 2 * k:2 * k + 2], tok_w[:, 2 * k:2 * k + 2]).then_inc(tokw_in[k], 16)
                load_patches(0, k)
            sp.dma_start(small_sb[:], small).then_inc(small_in, 16)
            sp.dma_start(const_sb[:], consts).then_inc(const_in, 16)
            load_qkv(0)
            load_patches(1, 0)
            load_qkv(1)
            for k in range(1, KP // 2):
                load_patches(1, k)
            for m in range(2, 6):
                load_qkv(m)
            sp.dma_start(w_out_sb[:], w_out).then_inc(wout_in, 16)
            sp.dma_start(w1_sb[:].rearrange("p (e f) -> p e f", e=E), w1).then_inc(w1_in, 16)
            sp.dma_start(w2_sb[:], w2).then_inc(w2_in, 16)
            for half in range(2):
                sp.wait_ge(y_ready, half + 1)
                sp.dma_start(out[:, half * HT:(half + 1) * HT], y[:, half]).then_inc(stored, 16)
            sp.wait_ge(stored, 32)


def constants(S):
    import numpy as np

    row, col = np.arange(S)[:, None], np.arange(S)[None, :]
    scale = np.float32(64) ** -0.5
    masks = np.zeros((P, 3, S), np.float32)
    for base in (0, 64):
        masks[base:base + S, 0] = np.where(row <= col, scale, 0)
        masks[base:base + S, 1] = np.where(row > col, 0.5, 0)
        masks[base:base + S, 2] = np.where(col <= row, 0, NEG)
    center = np.eye(P) - 1.0 / P
    return np.concatenate([center, np.eye(P), masks.reshape(P, 3 * S)], axis=1).astype(np.float32)


def kernel(**inputs):
    import numpy as np
    import concourse.bacc as bacc
    from concourse.bass_utils import run_bass_kernel_spmd

    x = np.asarray(inputs["x"])
    B, C, H, W = x.shape
    pz = 16
    D = inputs["L0_tok_w"].shape[0]
    hp, wp = H // pz, W // pz
    S = hp * wp
    E, _, DFF = inputs["L0_ffn_W1"].shape
    K = C * pz * pz
    KP = K // P
    HD = inputs["L0_attn_w_q_u"].shape[1]
    dims = dict(B=B, S=S, D=D, HEADS=HD // 64, DH=64, E=E, DFF=DFF, KP=KP)

    def a(name):
        return np.asarray(inputs[name])

    patches = x.reshape(B, C, hp, pz, wp, pz).transpose(1, 3, 5, 0, 2, 4).reshape(KP, P, B * S).transpose(1, 0, 2)
    tok_w = a("L0_tok_w").T.reshape(KP, P, D).transpose(1, 0, 2)
    small = np.concatenate([a("L0_tok_b").reshape(P, 1), a("L0_ffn_b2").T, a("L0_ffn_Wg"),
                            a("L0_ffn_b1").reshape(E * DFF // P, P).T], axis=1)
    arrays = {
        "patches": patches, "tok_w": tok_w, "consts": constants(S), "small": small,
        "w_out": a("L0_attn_w_out").reshape(HD // P, P, D).transpose(1, 0, 2),
        "w1": a("L0_ffn_W1").transpose(1, 0, 2),
        "w2": a("L0_ffn_W2").reshape(E * DFF // P, P, D).transpose(1, 0, 2).reshape(P, E * DFF),
    }
    for n in ("q_u", "k_u", "v_u", "q_c", "k_c", "v_c"):
        arrays[f"w_{n}"] = a(f"L0_attn_w_{n}")
    arrays = {k: np.ascontiguousarray(v) for k, v in arrays.items()}
    nc = bacc.Bacc("TRN2", target_bir_lowering=False, num_devices=1)
    ap = {k: nc.dram_tensor(k, v.shape, mybir.dt.from_np(v.dtype), kind="ExternalInput").ap() for k, v in arrays.items()}
    out = nc.dram_tensor("out", (D, B * S), F32, kind="ExternalOutput").ap()
    vit_layer(nc, ap["patches"], ap["tok_w"], ap["consts"], ap["small"],
              [ap[f"w_{n}"] for n in ("q_u", "k_u", "v_u", "q_c", "k_c", "v_c")],
              ap["w_out"], ap["w1"], ap["w2"], out, dims)
    r = run_bass_kernel_spmd(nc, [arrays], core_ids=[0])
    return r.results[0]["out"].T.reshape(B, S, D)
```
